# Optimizing a Trainium2 kernel written in Bass

```python
import numpy as np
import jax
import jax.numpy as jnp

def _softmax(x, axis=-1):
    return jax.nn.softmax(x, axis=axis)

def _gelu(x):
    return jax.nn.gelu(x, approximate=True)

def _silu(x):
    return jax.nn.silu(x)

def _sigmoid(x):
    return jax.nn.sigmoid(x)

def _layernorm(x, axis=-1, eps=1e-05):
    m = jnp.mean(x, axis=axis, keepdims=True)
    v = jnp.var(x, axis=axis, keepdims=True)
    return (x - m) / jnp.sqrt(v + eps)

def _scatter_add(tgt, idx, src, axis=0):
    return tgt.at[idx].add(src)

def _segment_sum(src, seg, n):
    return jax.ops.segment_sum(src, seg, n)
kernel_name = 'mk_adaln_d1_jaxref_r4_08cac4'

def setup_inputs(seed: int=0):
    np.random.seed(seed)
    _w = jnp.asarray

    def _L0_attn_setup():
        import jax, jax.numpy as jnp
        import numpy as np
        ROPE_DIM = 64
        GN_GROUPS = 32
        GN_CHANNELS = 512
        GN_EPS = 1e-05

        def rope_rotate(x):
            T = x.shape[-2]
            inv_freq = 1.0 / 10000.0 ** (jnp.arange(0, ROPE_DIM, 2, dtype=jnp.float32) / ROPE_DIM)
            freqs = jnp.arange(T, dtype=jnp.float32)[:, None] * inv_freq[None, :]
            freqs = jnp.repeat(freqs, 2, axis=-1)
            cos, sin = (jnp.cos(freqs), jnp.sin(freqs))
            xr = x[..., :ROPE_DIM]
            x1, x2 = (xr[..., 0::2], xr[..., 1::2])
            rot = jnp.stack((-x2, x1), axis=-1).reshape(xr.shape)
            xr = xr * cos + rot * sin
            return jnp.concatenate([xr, x[..., ROPE_DIM:]], axis=-1)

        def group_norm_rows(x2d, weight, bias):
            N, Cc = x2d.shape
            xg = x2d.reshape(N, GN_GROUPS, Cc // GN_GROUPS)
            mu = xg.mean(-1, keepdims=True)
            var = xg.var(-1, keepdims=True)
            xn = ((xg - mu) * jax.lax.rsqrt(var + GN_EPS)).reshape(N, Cc)
            return xn * weight + bias

        def _reference_tuple_inner(X, S_n, W_Q, hh_b, gn_weight, gn_bias):
            B, T, _ = X.shape
            Q = jax.nn.relu(rope_rotate(X @ W_Q))
            H = jnp.tanh(Q + hh_b)
            C = H.shape[-1]
            out = group_norm_rows(H.reshape(-1, C), gn_weight, gn_bias).reshape(B, T, C)
            out = jnp.swapaxes(out, -2, -1).reshape(B, T, C)
            return (out, S_n)
        key = jax.random.key(seed)
        ks = jax.random.split(key, 4)
        B, T, I, C = (2, 1024, 512, 512)
        X = jax.random.normal(ks[0], (B, T, I), dtype=jnp.float32)
        S_n = jnp.zeros((B, C), dtype=jnp.float32)
        W_Q = jax.random.normal(ks[1], (I, C), dtype=jnp.float32) / I
        hh_b = jax.random.normal(ks[2], (C,), dtype=jnp.float32) * 0.02
        gn_weight = jnp.ones((C,), dtype=jnp.float32)
        gn_bias = jnp.zeros((C,), dtype=jnp.float32)
        return {'X': X, 'S_n': S_n, 'W_Q': W_Q, 'hh_b': hh_b, 'gn_weight': gn_weight, 'gn_bias': gn_bias}
    _L0_attn_in = _L0_attn_setup()

    def _L0_ffn_setup():
        import jax, jax.numpy as jnp
        import numpy as np
        HIDDEN = 512
        INTER = 1376
        LUT_SIZE = 16

        def _ghost_linear(x, idx, lut):
            w = lut[idx]
            return jnp.einsum('bsh,oh->bso', x, w)
        key = jax.random.key(seed)
        k_x, k_lut, k_g, k_u, k_d = jax.random.split(key, 5)
        x = jax.random.normal(k_x, (2, 1024, HIDDEN), dtype=jnp.float32)
        lut = jax.random.normal(k_lut, (LUT_SIZE,), dtype=jnp.float32) * 0.02
        gate_idx = jax.random.randint(k_g, (INTER, HIDDEN), 0, LUT_SIZE, dtype=jnp.int32)
        up_idx = jax.random.randint(k_u, (INTER, HIDDEN), 0, LUT_SIZE, dtype=jnp.int32)
        down_idx = jax.random.randint(k_d, (HIDDEN, INTER), 0, LUT_SIZE, dtype=jnp.int32)
        return {'x': x, 'lut': lut, 'gate_idx': gate_idx, 'up_idx': up_idx, 'down_idx': down_idx}
    _L0_ffn_in = _L0_ffn_setup()
    _L0_c = _w((lambda *s: np.random.randn(*s).astype(np.float32) * 0.05)(2, 512))
    _L0_wmod = _w((lambda *s: np.random.randn(*s).astype(np.float32) * 0.05)(512, 6 * 512) * 512 ** (-0.5))
    _d = {'L0_attn_X': _L0_attn_in['X'], 'L0_attn_S_n': _L0_attn_in['S_n'], 'L0_attn_W_Q': _L0_attn_in['W_Q'], 'L0_attn_hh_b': _L0_attn_in['hh_b'], 'L0_attn_gn_weight': _L0_attn_in['gn_weight'], 'L0_attn_gn_bias': _L0_attn_in['gn_bias'], 'L0_ffn_lut': _L0_ffn_in['lut'], 'L0_ffn_gate_idx': _L0_ffn_in['gate_idx'], 'L0_ffn_up_idx': _L0_ffn_in['up_idx'], 'L0_ffn_down_idx': _L0_ffn_in['down_idx'], 'L0_c': _L0_c, 'L0_wmod': _L0_wmod}
    _x0 = _d['L0_attn_X']
    _d['L0_attn_X'] = jax.random.normal(jax.random.fold_in(jax.random.key(seed), 1), (2, 2048, 512), dtype=_x0.dtype)
    del _x0
    return _d

def reference(L0_attn_X, L0_attn_S_n, L0_attn_W_Q, L0_attn_hh_b, L0_attn_gn_weight, L0_attn_gn_bias, L0_ffn_lut, L0_ffn_gate_idx, L0_ffn_up_idx, L0_ffn_down_idx, L0_c, L0_wmod):

    def _L0_attn_ref(X, S_n, W_Q, hh_b, gn_weight, gn_bias):
        import jax, jax.numpy as jnp
        import numpy as np
        ROPE_DIM = 64
        GN_GROUPS = 32
        GN_CHANNELS = 512
        GN_EPS = 1e-05

        def rope_rotate(x):
            T = x.shape[-2]
            inv_freq = 1.0 / 10000.0 ** (jnp.arange(0, ROPE_DIM, 2, dtype=jnp.float32) / ROPE_DIM)
            freqs = jnp.arange(T, dtype=jnp.float32)[:, None] * inv_freq[None, :]
            freqs = jnp.repeat(freqs, 2, axis=-1)
            cos, sin = (jnp.cos(freqs), jnp.sin(freqs))
            xr = x[..., :ROPE_DIM]
            x1, x2 = (xr[..., 0::2], xr[..., 1::2])
            rot = jnp.stack((-x2, x1), axis=-1).reshape(xr.shape)
            xr = xr * cos + rot * sin
            return jnp.concatenate([xr, x[..., ROPE_DIM:]], axis=-1)

        def group_norm_rows(x2d, weight, bias):
            N, Cc = x2d.shape
            xg = x2d.reshape(N, GN_GROUPS, Cc // GN_GROUPS)
            mu = xg.mean(-1, keepdims=True)
            var = xg.var(-1, keepdims=True)
            xn = ((xg - mu) * jax.lax.rsqrt(var + GN_EPS)).reshape(N, Cc)
            return xn * weight + bias

        def _reference_tuple_inner(X, S_n, W_Q, hh_b, gn_weight, gn_bias):
            B, T, _ = X.shape
            Q = jax.nn.relu(rope_rotate(X @ W_Q))
            H = jnp.tanh(Q + hh_b)
            C = H.shape[-1]
            out = group_norm_rows(H.reshape(-1, C), gn_weight, gn_bias).reshape(B, T, C)
            out = jnp.swapaxes(out, -2, -1).reshape(B, T, C)
            return (out, S_n)
        return _reference_tuple_inner(X, S_n, W_Q, hh_b, gn_weight, gn_bias)[0]

    def _L0_ffn_ref(x, lut, gate_idx, up_idx, down_idx):
        import jax, jax.numpy as jnp
        import numpy as np
        HIDDEN = 512
        INTER = 1376
        LUT_SIZE = 16

        def _ghost_linear(x, idx, lut):
            w = lut[idx]
            return jnp.einsum('bsh,oh->bso', x, w)
        gate = _ghost_linear(x, gate_idx, lut)
        up = _ghost_linear(x, up_idx, lut)
        h = jax.nn.silu(gate) * up
        return _ghost_linear(h, down_idx, lut)
    x = L0_attn_X
    mod = (_silu(L0_c) @ L0_wmod).reshape(L0_c.shape[0], 6, 1, -1)
    sa, ca, ga, sb, cb, gb = (mod[:, 0], mod[:, 1], mod[:, 2], mod[:, 3], mod[:, 4], mod[:, 5])
    ga = (2 * (ga >= 0) - 1) * jnp.maximum(jnp.abs(ga), 0.25)
    gb = (2 * (gb >= 0) - 1) * jnp.maximum(jnp.abs(gb), 0.25)
    h = _layernorm(x, axis=-1) * (1 + ca) + sa
    x = x + ga * _L0_attn_ref(h, L0_attn_S_n, L0_attn_W_Q, L0_attn_hh_b, L0_attn_gn_weight, L0_attn_gn_bias)
    h = _layernorm(x, axis=-1) * (1 + cb) + sb
    x = x + gb * _L0_ffn_ref(h, L0_ffn_lut, L0_ffn_gate_idx, L0_ffn_up_idx, L0_ffn_down_idx)
    return x

_drawn_inputs = setup_inputs


def setup_inputs(seed=0):
    import zlib

    import numpy as np

    out = dict(_drawn_inputs(seed))
    spreads = {'L0_attn_S_n': (0.0, 0.1),
     'L0_attn_gn_weight': (1.0, 0.2),
     'L0_attn_gn_bias': (0.0, 0.341)}
    factors = {}
    for name, (base, spread) in spreads.items():
        noise = np.random.default_rng([zlib.crc32(name.encode()), seed]).standard_normal(out[name].shape)
        drawn = base * np.exp(spread * noise) if base else spread * noise
        out[name] = jnp.asarray(drawn.astype(out[name].dtype))
    for name, factor in factors.items():
        out[name] = (out[name] * factor).astype(out[name].dtype)
    return out
```

```python
from contextlib import ExitStack, contextmanager

import numpy as np

import concourse.bass as bass
from concourse import mybir

F32 = mybir.dt.float32
F16 = mybir.dt.float16
I32 = mybir.dt.int32
ALU = mybir.AluOpType
ACT = mybir.ActivationFunctionType
AX = mybir.AxisListType.X
RMAX = bass.bass_isa.ReduceOp.max

P = 128
BATCH, T, C = 2, 2048, 512
BLK = 512
A = BLK // P
K = C // P
NB = T // BLK
F = 1376
J = -(-F // P)
F_LAST = F - (J - 1) * P
GRP, GSZ = 32, 16
ROPE = 64
S = 2
G = BATCH * NB // S
LUT = 16
EPS = 1e-5
RSQRT_SEED = float(0x5F3759DF)
EXP1 = float(1 << 23)
SA, CA, GA, SB, CB, GB = range(6)
SPLIT = ((0, 0), (0, 1), (1, 0))


class Steps:

    def __init__(self, eng, sem):
        self.eng, self.sem, self.base, self.n = eng, sem, 0, 0

    def step(self, ins):
        ins.then_inc(self.sem, 1)
        self.n += 1
        self.eng.wait_ge(self.sem, self.base + self.n)

    @contextmanager
    def loop(self, first, end, per):
        start = self.base + self.n
        with self.eng.Fori(first, end) as i:
            self.base, self.n = start + (i - first) * per, 0
            yield i
            assert self.n == per, self.n
        self.base, self.n = start + (end - first) * per, 0


def reach(eng, sem, value):
    if not isinstance(value, int) or value > 0:
        eng.wait_ge(sem, value)


def build(nc, x, wq, hh_b, gn_w, gn_b, lut, idx, c_t, wmod, cos, sin, out):
    x2_dram = nc.dram_tensor("x2_dram", (BATCH, NB, P, A * C), F32, kind="Internal").ap()
    x_rows = x.rearrange("b (m p q) n -> b m p q n", p=P, q=A)
    x_toks = x.rearrange("b (m a p) n -> b m p a n", p=P, a=A)
    x2_rows = x2_dram.rearrange("b m p (q n) -> b m p q n", q=A)
    out_rows = out.rearrange("b (m p q) n -> b m p q n", p=P, q=A)

    with ExitStack() as ctx:
        def sb(name, shape, dt):
            return ctx.enter_context(nc.sbuf_tensor(name, shape, dt))

        def sem(name):
            return ctx.enter_context(nc.semaphore(name))

        w_all = sb("w_all", [P, 2 * 3 * J * BLK], F16)
        W = [w_all[:, h * 3 * J * BLK:(h + 1) * 3 * J * BLK] for h in range(2)]
        mod_w = w_all[:, 0:2 * 6 * K * C].bitcast(F32).rearrange("p (s k n) -> p s k n", s=6, k=K)
        hid = [sb(f"hid{h}", [P, J * S * BLK], F16) for h in range(2)]
        h2 = [sb(f"h2_{h}", [P, S, K, BLK], F16) for h in range(2)]
        work = sb("work", [P, 2 * A * C], F32)
        H = work[:, 0:A * C].rearrange("p (a n) -> p a n", a=A)
        hq_all = work[:, A * C:2 * A * C].bitcast(F16)
        hq = [hq_all[:, h * K * BLK:(h + 1) * K * BLK].rearrange("p (k n) -> p k n", k=K) for h in range(2)]
        R = [sb(f"R{i}", [P, A * C], F32) for i in range(2)]
        xa = sb("xa", [P, A, C], F32)
        h32 = sb("h32", [P, 2, BLK], F32)
        sq = sb("sq", [P, 2, BLK], F32)
        WQ = [sb(f"WQ{h}", [P, K, C], F16) for h in range(2)]
        cosT = sb("cosT", [P, T // P * (ROPE // 2)], F32)
        sinT = sb("sinT", [P, T // P * (ROPE // 2)], F32)
        hhS = sb("hhS", [P, C], F32)
        gaB = sb("gaB", [P, BATCH, C], F32)
        gbB = sb("gbB", [P, BATCH, C], F32)
        sg = sb("sg", [P, S, BLK], F32)
        ident = sb("ident", [P, P], F32)
        vec = sb("vec", [P, 5, K, BATCH], F32)
        gnw = sb("gnw", [P, K], F32)
        gnb = sb("gnb", [P, K], F32)
        cT = sb("cT", [P, K, BATCH], F32)
        lutS = sb("lutS", [P, LUT], F32)
        lutD = sb("lutD", [P, LUT // 2], F32)
        st = sb("st", [P, A, 6], F32)
        mv = sb("mv", [P, A, 2], F32)
        ls = sb("ls", [P, 5, A], F32)
        gs = sb("gs", [P, 4, A * GRP], F32)
        col = sb("col", [P, 16], F32)
        hd = sb("hd", [P, S, BLK], F32)
        ps = ctx.enter_context(nc.psum_tensor("ps", [P, 8 * BLK], F32))

        def bank(i):
            return ps[:, i * BLK:(i + 1) * BLK]

        GU, TB, QY, MASK = (0, 1, 2, 3), (4, 5), (6, 7), (4, 5, 6)
        idxb = [h32[:, i, :].bitcast(I32) for i in range(2)]
        bit = [sq[:, i, :].bitcast(I32) for i in range(2)]
        pairs = [work[:, :].rearrange("p (g n) -> p g n", n=BLK)[:, g, :] for g in range(8)], \
                [R[g // 4][:, g % 4 * BLK:(g % 4 + 1) * BLK] for g in range(8)]
        (c_wqmax, c_wqall, c_sq, c_isq, c_s, c_is, c_sh, c_kappa, c_kappa2, c_e, c_tmp) = \
            (col[:, i:i + 1] for i in range(11))

        x_in = sem("x_in"); rows_in = [sem("rows_in0"), sem("rows_in1")]
        wq_in = sem("wq_in"); const_in = sem("const_in"); rope_in = sem("rope_in")
        mod_in = [sem(f"mod_in{s}") for s in range(6)]
        idx_in = [sem("idx_in0"), sem("idx_in1")]
        x2_out = sem("x2_out"); y_out = sem("y_out")
        id_zero = sem("id_zero"); id_ready = sem("id_ready"); wq_all = sem("wq_all")
        dstep = sem("dstep"); astep = sem("astep")
        silu_c = sem("silu_c"); vec_mm = sem("vec_mm"); row_mm = sem("row_mm")
        vec_ready = sem("vec_ready"); row_ready = sem("row_ready")
        wq_max = sem("wq_max"); wq_ready = sem("wq_ready"); scales_ready = sem("scales_ready")
        ln_stats = sem("ln_stats"); xn_ready = sem("xn_ready"); xt_ready = sem("xt_ready")
        h32_ready = sem("h32_ready"); hi_ready = sem("hi_ready"); lo_ready = sem("lo_ready")
        q_ready = sem("q_ready"); q_taken = sem("q_taken"); pre_tanh = sem("pre_tanh"); tanh_ready = sem("tanh_ready")
        centered = sem("centered"); squared = sem("squared"); sq_summed = sem("sq_summed")
        g_ready = sem("g_ready"); gt_ready = sem("gt_ready"); x2_ready = sem("x2_ready")
        bit_ready = sem("bit_ready"); pairs_ready = sem("pairs_ready"); w_built = sem("w_built")
        gu_ready = sem("gu_ready"); silu_ready = sem("silu_ready"); hd_ready = sem("hd_ready")
        hid_hi_ready = sem("hid_hi_ready"); hid_ready = sem("hid_ready")
        y_ready = sem("y_ready"); o_ready = sem("o_ready")

        block = ctx.enter_context(nc.Block())

        LN_A = [0, 1, 2, 3, 8, 9, 10, 11]
        LN_B = [4, 5, 6, 7, 12, 13, 14, 15]
        R_A = [0, 1, 2, 3, 6, 7, 8, 9]
        R_D = [4, 5, 10, 11, 12, 13, 14, 15]

        @block.sync
        def _(sp):
            def load_x(src, m):
                reach(sp, xt_ready, 4 * m)
                sp.dma_start(xa[:], src).then_inc(x_in, 16)

            def load_rows(r, src, count):
                sp.dma_start(R[r].rearrange("p (q n) -> p q n", q=A), src).then_inc(rows_in[r], 16)

            def rows_of_block(b, q):
                return x.rearrange("b (m p q) n -> b q p m n", p=P, q=A)[b, q]

            def x2_of_block(b, q):
                return x2_dram.rearrange("b m p (q n) -> b q p m n", q=A)[b, q]

            sp.dma_start(cT[:], c_t).then_inc(const_in, 16)
            sp.dma_start(lutS[:], lut.partition_broadcast(P)).then_inc(const_in, 16)
            sp.dma_start(hhS[:], hh_b.partition_broadcast(P)).then_inc(const_in, 16)
            sp.dma_start(gnw[:], gn_w).then_inc(const_in, 16)
            sp.dma_start(gnb[:], gn_b).then_inc(const_in, 16)
            load_x(x_toks[0, 0], 0)
            wq_f32 = hid[0][:, 0:2 * K * C].bitcast(F32).rearrange("p (k n) -> p k n", k=K)
            sp.dma_start(wq_f32, wq.rearrange("(k p) n -> p k n", p=P)).then_inc(wq_in, 16)
            mod_v = wmod.rearrange("(k p) (s n) -> s p k n", p=P, s=6)
            for s in (SA, CA, GA):
                sp.dma_start(mod_w[:, s], mod_v[s]).then_inc(mod_in[s], 16)
            sp.dma_start(cosT[:], cos).then_inc(rope_in, 16)
            sp.dma_start(sinT[:], sin).then_inc(rope_in, 16)
            load_rows(0, rows_of_block(0, 0), 0)
            for s in (SB, CB, GB):
                sp.dma_start(mod_w[:, s], mod_v[s]).then_inc(mod_in[s], 16)

            for q in range(NB):
                n = q
                if q + 1 < NB:
                    load_x(x_toks[0, q + 1], LN_A[n] + 1)
                    reach(sp, x2_out, 16 * n)
                    load_rows((n + 1) % 2, rows_of_block(0, q + 1), 0)
                sp.wait_ge(x2_ready, K * (n + 1))
                if n:
                    sp.wait_ge(x2_out, 16 * n)
                sp.dma_start(x2_of_block(0, q), R[n % 2].rearrange("p (q n) -> p q n", q=A)).then_inc(x2_out, 16)
            sp.wait_ge(x2_out, 16 * NB)
            for s in range(S + 1):
                load_x(x2_rows[0, s], LN_B[s])
            for w in range(2):
                if w == 0:
                    sp.wait_ge(lo_ready, K * (LN_B[S - 1] + 1))
                sp.dma_start(idxb[w], idx[w]).then_inc(idx_in[w], 16)
            with sp.Fori(1, (3 * J + 1) // 2) as i:
                for w in range(2):
                    sp.wait_ge(w_built, 2 * i + w - 1)
                    sp.dma_start(idxb[w], idx[bass.ds(2 * i + w, 1)].squeeze(0)).then_inc(idx_in[w], 16)

            def load_ffn_block(blk):
                load_x(x2_rows[blk // NB, blk % NB], LN_B[blk])

            def down_io(g):
                b = g * S // NB
                if g + 1 < G:
                    load_ffn_block((g + 1) * S + 1)
                for s in range(S):
                    r = R_D[g * S + s]
                    m = (g * S + s) % NB
                    with sp.Fori(0, A) as q:
                        d = (g * S + s) * A + q
                        sp.wait_ge(o_ready, d + 1)
                        sp.dma_start(out_rows[b, m, :, bass.ds(q, 1), :].squeeze(1),
                                     R[r % 2][:, bass.ds(q * C, C)]).then_inc(y_out, 16)
                    sp.wait_ge(y_out, 16 * (g * S + s + 1) * A)

            def load_down_rows(g, s):
                b = g * S // NB
                load_rows(R_D[g * S + s] % 2, x2_rows[b, (g * S + s) % NB], 0)

            for g in range(G):
                if g == 1:
                    for q in range(NB):
                        n = NB + q
                        if q == 0:
                            load_x(x_toks[1, 0], LN_A[n])
                            load_rows(R_A[n] % 2, rows_of_block(1, 0), 0)
                        if q + 1 < NB:
                            load_x(x_toks[1, q + 1], LN_A[n] + 1)
                            reach(sp, x2_out, 16 * n)
                            load_rows(R_A[n + 1] % 2, rows_of_block(1, q + 1), 0)
                        sp.wait_ge(x2_ready, K * (n + 1))
                        sp.wait_ge(x2_out, 16 * n)
                        sp.dma_start(x2_of_block(1, q), R[R_A[n] % 2].rearrange("p (q n) -> p q n", q=A)).then_inc(x2_out, 16)
                    sp.wait_ge(x2_out, 16 * BATCH * NB)
                    load_ffn_block(2 * S)
                if g == 2:
                    load_ffn_block(3 * S)
                if g == 0:
                    sp.wait_ge(w_built, 3 * J)
                for s in range(S):
                    load_down_rows(g, s)
                down_io(g)

        @block.gpsimd
        def _(pool):
            nc.gpsimd.memset(ident[:], 0.0).then_inc(id_zero, 1)
            pool.wait_ge(id_zero, 1)
            nc.gpsimd.affine_select(out=ident[:], in_=ident[:], compare_op=ALU.not_equal, fill=1.0, base=0,
                                    pattern=[[-1, P]], channel_multiplier=1).then_inc(id_ready, 1)
            pool.wait_ge(wq_max, 1)
            nc.gpsimd.partition_all_reduce(c_wqall, c_wqmax, P, RMAX).then_inc(wq_all, 1)

        @block.scalar
        def _(act):
            def norm(m):
                act.wait_ge(ln_stats, m + 1)
                for a in range(A):
                    ins = nc.scalar.activation(xa[:, a], xa[:, a], ACT.Identity,
                                               bias=ls[:, 3, a:a + 1], scale=ls[:, 2, a:a + 1])
                ins.then_inc(xn_ready, 1)

            def affine(m, scale, shift, b, dest, dest_free):
                for k in range(K):
                    act.wait_ge(xt_ready, K * m + k + 1)
                    reach(act, lo_ready, K * m + max(k - 1, 0))
                    nc.scalar.activation(h32[:, k % 2], bank(TB[k % 2]), ACT.Identity,
                                         bias=vec[:, shift, k, b:b + 1], scale=vec[:, scale, k, b:b + 1]) \
                      .then_inc(h32_ready, 1)
                    act.wait_ge(h32_ready, K * m + k + 1)
                    if k == 0:
                        dest_free()
                    nc.scalar.activation(dest[:, k], h32[:, k % 2], ACT.Copy).then_inc(hi_ready, 1)

            def tanh(n, a):
                act.wait_ge(pre_tanh, A * n + a + 1)
                nc.scalar.activation(H[:, a], H[:, a], ACT.Tanh, scale=c_isq).then_inc(tanh_ready, 1)

            def square(n, a):
                act.wait_ge(centered, A * n + a + 1)
                reach(act, sq_summed, A * n + max(a - 1, 0))
                nc.scalar.activation(sq[:, a % 2], H[:, a], ACT.Square).then_inc(squared, 1)

            def silu(g, j, s):
                u = (g * J + j) * S + s
                act.wait_ge(gu_ready, u + 1)
                reach(act, hd_ready, u - 1 if g or s else u)
                nc.scalar.activation(sg[:, s], bank(GU[2 * s]), ACT.Silu, scale=c_is).then_inc(silu_ready, 1)

            def hid_hi(g, j, s):
                u = (g * J + j) * S + s
                act.wait_ge(hd_ready, u + 1)
                nc.scalar.activation(hid[0][:, bass.ds((j * S + s) * BLK, BLK)], hd[:, s], ACT.Copy) \
                  .then_inc(hid_hi_ready, 1)

            def pair_tables(w, par):
                act.wait_ge(bit_ready, w + 1)
                reach(act, w_built, w - 1)
                for g in range(8):
                    ins = nc.scalar.activation(pairs[par][g], bit[par], ACT.Identity,
                                               bias=lutS[:, 2 * g:2 * g + 1], scale=lutD[:, g:g + 1])
                ins.then_inc(pairs_ready, 1)

            act.wait_ge(const_in, 80)
            nc.scalar.activation(cT[:], cT[:], ACT.Silu).then_inc(silu_c, 1)

            act.wait_ge(vec_ready, 1)
            with act.Fori(0, NB) as q:
                norm(q)
                affine(q, CA, SA, 0, hq[0], lambda: act.wait_ge(q_ready, A * q))
                tanh(q, 0); tanh(q, 1); square(q, 0); tanh(q, 2)
                square(q, 1); tanh(q, 3); square(q, 2); square(q, 3)

            act.wait_ge(vec_ready, 2)
            for s in range(S):
                norm(LN_B[s])
                affine(LN_B[s], CB, SB, 0, h2[0][:, s], lambda: None)
            norm(LN_B[S])

            for w in range(3):
                pair_tables(w, w % 2)
            with act.Fori(0, (J - 1) // 2) as it:
                for jj in range(2):
                    for t in range(3):
                        w = 3 + 3 * jj + t
                        pair_tables(6 * it + w, w % 2)
                    j = 2 * it + jj
                    silu(0, j, 0); silu(0, j, 1); hid_hi(0, j, 0); hid_hi(0, j, 1)
            silu(0, J - 1, 0); silu(0, J - 1, 1); hid_hi(0, J - 1, 0); hid_hi(0, J - 1, 1)

            for g in range(G):
                if g == 1:
                    with act.Fori(0, NB) as q:
                        n, m = NB + q, LN_A[NB] + q
                        norm(m)
                        silu(g, 2 * q, 0); hid_hi(g, 2 * q, 0)
                        affine(m, CA, SA, 1, hq[0], lambda: act.wait_ge(q_ready, A * n))
                        silu(g, 2 * q, 1); hid_hi(g, 2 * q, 1)
                        tanh(n, 0); tanh(n, 1); square(n, 0); tanh(n, 2)
                        square(n, 1); tanh(n, 3); square(n, 2); square(n, 3)
                        silu(g, 2 * q + 1, 0); hid_hi(g, 2 * q + 1, 0)
                        silu(g, 2 * q + 1, 1); hid_hi(g, 2 * q + 1, 1)
                if g > 0:
                    if g + 1 < G:
                        norm(LN_B[(g + 1) * S])
                    with act.Fori(2 * NB if g == 1 else 0, J) as j:
                        for s in range(S):
                            silu(g, j, s)
                            hid_hi(g, j, s)
                if g + 1 < G:
                    for s in range(S):
                        blk = (g + 1) * S + s
                        if s:
                            norm(LN_B[blk])
                        affine(LN_B[blk], CB, SB, blk // NB, h2[0][:, s], lambda: None)

        @block.vector
        def _(dve):
            steps = Steps(dve, dstep)
            step = steps.step
            v = nc.vector

            def alone():
                v.memset(col[:, 15:16], 0.0)

            def rsqrt(x_, t_, y_):
                step(v.tensor_scalar(t_.bitcast(I32), x_.bitcast(I32), 1, None, ALU.logical_shift_right))
                step(v.tensor_scalar(y_.bitcast(I32), t_.bitcast(I32), -1.0, RSQRT_SEED, ALU.mult, ALU.add))
                for _ in range(3):
                    step(v.tensor_tensor(t_, y_, y_, ALU.mult))
                    step(v.scalar_tensor_tensor(t_, t_, -0.5, x_, ALU.mult, ALU.mult))
                    step(v.scalar_tensor_tensor(y_, t_, 1.5, y_, ALU.add, ALU.mult))

            def stats(m):
                dve.wait_ge(x_in, 16 * m + 16)
                for a in range(A):
                    ins = v.bn_stats(st[:, a], xa[:, a])
                step(ins)
                alone()
                for a in range(A):
                    ins = v.bn_aggr(mv[:, a], st[:, a])
                step(ins)
                reach(dve, xn_ready, m)
                step(v.tensor_scalar(ls[:, 0], mv[:, :, 1], EPS, None, ALU.add))
                rsqrt(ls[:, 0], ls[:, 1], ls[:, 2])
                v.scalar_tensor_tensor(ls[:, 3], mv[:, :, 0], -1.0, ls[:, 2], ALU.mult, ALU.mult) \
                 .then_inc(ln_stats, 1)

            def split_lo(m, hi, lo):
                for k in range(K):
                    dve.wait_ge(hi_ready, K * m + k + 1)
                    v.tensor_tensor(lo[:, k], h32[:, k % 2], hi[:, k], ALU.subtract).then_inc(lo_ready, 1)

            def rope_relu(n, q, a):
                reach(dve, pre_tanh, A * n + a)
                dve.wait_ge(q_ready, A * n + a + 1)
                Q = bank(QY[a % 2])
                half = ROPE // 2
                at = (q * A + a) * half
                cs, sn = cosT[:, bass.ds(at, half)], sinT[:, bass.ds(at, half)]
                Qr = Q[:, 0:ROPE].rearrange("p (i e) -> p e i", e=2)
                rot2 = gs2[:, 0:ROPE].rearrange("p (i e) -> p e i", e=2)
                tmp2 = gs2[:, ROPE:2 * ROPE].rearrange("p (i e) -> p e i", e=2)
                for e in range(2):
                    v.tensor_tensor(rot2[:, e], Qr[:, e], cs, ALU.mult)
                v.tensor_tensor(tmp2[:, 0], Qr[:, 1], sn, ALU.mult)
                step(v.tensor_tensor(tmp2[:, 1], Qr[:, 0], sn, ALU.mult))
                v.tensor_tensor(rot2[:, 0], rot2[:, 0], tmp2[:, 0], ALU.subtract)
                step(v.tensor_tensor(rot2[:, 1], rot2[:, 1], tmp2[:, 1], ALU.add))
                v.scalar_tensor_tensor(H[:, a, ROPE:], Q[:, ROPE:], 0.0, hhS[:, ROPE:], ALU.max, ALU.add) \
                 .then_inc(q_taken, 1)
                v.scalar_tensor_tensor(H[:, a, 0:ROPE], gs2[:, 0:ROPE], 0.0, hhS[:, 0:ROPE],
                                       ALU.max, ALU.add).then_inc(pre_tanh, 1)

            def center(n, a):
                dve.wait_ge(tanh_ready, A * n + a + 1)
                Hg = H[:, a].rearrange("p (g e) -> p g e", e=GSZ)
                sums = gs[:, 0, a * GRP:(a + 1) * GRP]
                step(v.tensor_reduce(sums, Hg, axis=AX, op=ALU.add))
                step(v.tensor_scalar(sums, sums, 1.0 / GSZ, None, ALU.mult))
                v.tensor_tensor(Hg, Hg, sums.unsqueeze(2).broadcast_to((P, GRP, GSZ)), ALU.subtract) \
                 .then_inc(centered, 1)

            def sum_squares(n, a):
                dve.wait_ge(squared, A * n + a + 1)
                v.tensor_reduce(gs[:, 1, a * GRP:(a + 1) * GRP], sq[:, a % 2].rearrange("p (g e) -> p g e", e=GSZ),
                                axis=AX, op=ALU.add).then_inc(sq_summed, 1)

            def group_scale(n, b):
                dve.wait_ge(sq_summed, A * n + A)
                step(v.tensor_scalar(gs[:, 1], gs[:, 1], 1.0 / GSZ, EPS, ALU.mult, ALU.add))
                rsqrt(gs[:, 1], gs[:, 2], gs[:, 3])
                r = gs[:, 3].rearrange("p (a g) -> p a g", a=A)
                ga = vec[:, GA, :, b].unsqueeze(2).broadcast_to((P, A, GRP))
                step(v.tensor_tensor(r, r, ga, ALU.mult))
                Hg = H.rearrange("p a (g e) -> p (a g) e", e=GSZ)
                v.tensor_tensor(Hg, Hg, gs[:, 3].unsqueeze(2).broadcast_to((P, A * GRP, GSZ)), ALU.mult) \
                 .then_inc(g_ready, 1)

            def residual(n, b, r, loads):
                dve.wait_ge(rows_in[r], 16 * loads)
                for k in range(K):
                    Rk = R[r][:, k * C:(k + 1) * C]
                    ins = v.scalar_tensor_tensor(Rk, gaB[:, b], gnb[:, k:k + 1], Rk, ALU.mult, ALU.add)
                step(ins)
                for k in range(K):
                    Rk = R[r][:, k * C:(k + 1) * C]
                    dve.wait_ge(gt_ready, K * n + k + 1)
                    v.scalar_tensor_tensor(Rk, bank(TB[k % 2]), gnw[:, k:k + 1], Rk, ALU.mult, ALU.add) \
                     .then_inc(x2_ready, 1)

            def group_norm(n, q):
                rope_relu(n, q, 0); rope_relu(n, q, 1); center(n, 0); rope_relu(n, q, 2)
                center(n, 1); sum_squares(n, 0); rope_relu(n, q, 3); center(n, 2)
                sum_squares(n, 1); center(n, 3); sum_squares(n, 2); sum_squares(n, 3)

            def low_bit(w, par, count):
                dve.wait_ge(idx_in[par], 16 * count)
                v.tensor_scalar(bit[par], idxb[par], 1, None, ALU.bitwise_and).then_inc(bit_ready, 1)

            def build_chunk(w, par, slot, nxt):
                for i in range(3):
                    ins = v.tensor_scalar(bank(MASK[i]).bitcast(I32), idxb[par], 2 << i, None, ALU.bitwise_and)
                if nxt is not None:
                    step(ins)
                    low_bit(*nxt)
                else:
                    step(ins)
                dve.wait_ge(pairs_ready, w + 1)
                g = pairs[par]
                for level, span in ((0, 1), (1, 2), (2, 4)):
                    alone()
                    for at in range(0, 8, 2 * span):
                        ins = v.copy_predicated(g[at], bank(MASK[level]).bitcast(I32), g[at + span])
                    step(ins)
                hi, lo = (W[h][:, bass.ds(slot * BLK, BLK)] for h in range(2))
                step(v.tensor_scalar(hi, g[0], 1.0, None, ALU.mult))
                v.tensor_tensor(lo, g[0], hi, ALU.subtract).then_inc(w_built, 1)

            def hidden(g, j, s):
                u = (g * J + j) * S + s
                reach(dve, hid_ready, u - 1 if g or s else u)
                dve.wait_ge(silu_ready, u + 1)
                v.scalar_tensor_tensor(hd[:, s], bank(GU[2 * s + 1]), c_kappa, sg[:, s], ALU.mult, ALU.mult) \
                 .then_inc(hd_ready, 1)

            def hid_lo(g, j, s):
                u = (g * J + j) * S + s
                dve.wait_ge(hid_hi_ready, u + 1)
                at = bass.ds((j * S + s) * BLK, BLK)
                v.tensor_tensor(hid[1][:, at], hd[:, s], hid[0][:, at], ALU.subtract).then_inc(hid_ready, 1)

            def down_out(g, s, q, b, par):
                d = (g * S + s) * A + q
                r = R_D[g * S + s] % 2
                dve.wait_ge(y_ready, d + 1)
                step(v.scalar_tensor_tensor(hd[:, par], bank(QY[par]), c_kappa2, gbB[:, b], ALU.mult, ALU.mult))
                Rq = R[r][:, bass.ds(q * C, C)]
                v.tensor_tensor(Rq, hd[:, par], Rq, ALU.add).then_inc(o_ready, 1)

            dve.wait_ge(const_in, 80)
            gs2 = gs[:, 2]

            def magnitude(dst, src):
                step(v.tensor_scalar(dst.bitcast(I32), src.bitcast(I32), 0x7FFFFFFF, None, ALU.bitwise_and))

            def exponent(dst, src, lowest, highest):
                step(v.tensor_scalar(dst.bitcast(I32), src.bitcast(I32), 0x7F800000, None, ALU.bitwise_and))
                step(v.tensor_scalar(dst.bitcast(I32), dst.bitcast(I32), lowest * EXP1, highest * EXP1,
                                     ALU.max, ALU.min))

            def field(dst, src, times, plus):
                step(v.tensor_scalar(dst.bitcast(I32), src.bitcast(I32), float(times), plus * EXP1,
                                     ALU.mult, ALU.add))

            tmp16 = gs[:, 0, 0:LUT]
            magnitude(tmp16, lutS[:])
            step(v.tensor_reduce(c_tmp, tmp16, axis=AX, op=ALU.max))
            exponent(c_e, c_tmp, 60, 186)
            field(c_s, c_e, -1, 264)
            field(c_is, c_s, -1, 254)
            field(c_sh, c_e, -2, 374)
            field(c_tmp, c_sh, -1, 254)
            step(v.tensor_tensor(c_kappa, c_is, c_sh, ALU.mult))
            step(v.tensor_tensor(c_kappa2, c_is, c_tmp, ALU.mult))
            step(v.tensor_scalar(lutS[:], lutS[:], c_s, None, ALU.mult))
            lp = lutS.rearrange("p (g e) -> p e g", e=2)
            v.tensor_tensor(lutD[:], lp[:, 1], lp[:, 0], ALU.subtract)

            wq_f32 = hid[0][:, 0:2 * K * C].bitcast(F32)
            wq_s = hid[1][:, 0:2 * K * C].bitcast(F32)
            dve.wait_ge(wq_in, 16)
            magnitude(wq_s, wq_f32)
            v.tensor_reduce(c_wqmax, wq_s, axis=AX, op=ALU.max).then_inc(wq_max, 1)
            stats(0)
            dve.wait_ge(wq_all, 1)
            exponent(c_e, c_wqall, 60, 186)
            field(c_sq, c_e, -1, 264)
            field(c_isq, c_sq, -1, 254)
            v.tensor_scalar(hhS[:], hhS[:], c_sq, None, ALU.mult)
            step(v.tensor_scalar(wq_s, wq_f32, c_sq, None, ALU.mult))
            step(v.tensor_scalar(WQ[0].rearrange("p k n -> p (k n)"), wq_s, 1.0, None, ALU.mult))
            v.tensor_tensor(WQ[1].rearrange("p k n -> p (k n)"), wq_s, WQ[0].rearrange("p k n -> p (k n)"),
                            ALU.subtract).then_inc(wq_ready, 1)

            vps = bank(QY[1])[:, 0:5 * K * BATCH].rearrange("p (s k b) -> p s k b", s=5, k=K)

            def gate_of(dst, src, tmp, tmp2):
                v.tensor_scalar(tmp, src, 0.0, 2.0, ALU.is_ge, ALU.mult)
                magnitude(tmp2, src)
                step(v.tensor_scalar(tmp2, tmp2, 0.25, None, ALU.max))
                return v.scalar_tensor_tensor(dst, tmp, 1.0, tmp2, ALU.subtract, ALU.mult)

            dve.wait_ge(vec_mm, 1)
            v.tensor_copy(vec[:, SA], vps[:, SA])
            v.tensor_scalar(vec[:, CA], vps[:, CA], 1.0, None, ALU.add)
            gv = vps[:, GA].rearrange("p k b -> p (k b)")
            gate_of(vec[:, GA].rearrange("p k b -> p (k b)"), gv, gs[:, 0, 0:K * BATCH], gs[:, 1, 0:K * BATCH]) \
                .then_inc(vec_ready, 1)
            for b in range(BATCH):
                dve.wait_ge(row_mm, b + 1)
                step(gate_of(gaB[:, b], bank(GU[b]), hd[:, 0], hd[:, 1]))
            dve.wait_ge(rope_in, 32)

            stats_steps, per_rope, per_center = 14, 2, 2
            per_a = 14 + 4 * 2 + 4 * 2 + 13 + 1
            with steps.loop(0, NB // 2, 2 * per_a) as it:
                for half in range(2):
                    q = 2 * it + half
                    split_lo(q, hq[0], hq[1])
                    group_norm(q, q)
                    group_scale(q, 0)
                    residual(q, 0, half, it + 1)
                    stats(q + 1)

            dve.wait_ge(vec_mm, 2)
            v.tensor_copy(vec[:, SB], vps[:, SB])
            v.tensor_scalar(vec[:, CB], vps[:, CB], 1.0, None, ALU.add).then_inc(vec_ready, 1)
            for b in range(BATCH):
                dve.wait_ge(row_mm, BATCH + b + 1)
                step(gate_of(gbB[:, b], bank(GU[2 + b]), hd[:, 0], hd[:, 1]))
            split_lo(LN_B[0], h2[0][:, 0], h2[1][:, 0])
            stats(LN_B[1])
            split_lo(LN_B[1], h2[0][:, 1], h2[1][:, 1])
            stats(LN_B[S])

            def slot_of(j, t):
                return 2 * j + t if t < 2 else 2 * J + j

            low_bit(0, 0, 1)
            for w in range(3):
                build_chunk(w, w % 2, slot_of(0, w), (w + 1, (w + 1) % 2, (w + 1) // 2 + 1))
            with steps.loop(0, (J - 1) // 2, 6 * 5) as it:
                for jj in range(2):
                    for t in range(3):
                        w = 3 + 3 * jj + t
                        build_chunk(6 * it + w, w % 2, slot_of(2 * it + 1 + jj, t),
                                    (6 * it + w + 1, (w + 1) % 2, 3 * it + (w + 1) // 2 + 1))
                    j = 2 * it + jj
                    hidden(0, j, 0); hidden(0, j, 1); hid_lo(0, j, 0); hid_lo(0, j, 1)
            for h in range(2):
                ins = v.memset(W[h][F_LAST:P, (3 * J - 1) * BLK:], 0.0)
            ins.then_inc(w_built, 1)
            hidden(0, J - 1, 0); hidden(0, J - 1, 1); hid_lo(0, J - 1, 0); hid_lo(0, J - 1, 1)

            for g in range(G):
                b = g * S // NB
                if g == 1:
                    stats(LN_A[NB])
                    with steps.loop(0, NB // 2, 2 * (4 * 2 + 4 * 2 + 13 + 1 + 14)) as it:
                        for half in range(2):
                            q = 2 * it + half
                            n, m = NB + q, LN_A[NB] + q
                            hidden(g, 2 * q, 0); hid_lo(g, 2 * q, 0)
                            split_lo(m, hq[0], hq[1])
                            hidden(g, 2 * q, 1); hid_lo(g, 2 * q, 1)
                            group_norm(n, q)
                            hidden(g, 2 * q + 1, 0); hid_lo(g, 2 * q + 1, 0)
                            group_scale(n, 1)
                            hidden(g, 2 * q + 1, 1); hid_lo(g, 2 * q + 1, 1)
                            residual(n, 1, half, 3 + it + 1)
                            stats(m + 1)
                if g > 0:
                    if g == 2:
                        stats(LN_B[(g + 1) * S])
                    with steps.loop(2 * NB if g == 1 else 0, J, 0) as j:
                        for s in range(S):
                            hidden(g, j, s)
                            hid_lo(g, j, s)
                for s in range(S):
                    blk, nxt = g * S + s, (g + 1) * S + s
                    if g + 1 < G:
                        split_lo(LN_B[nxt], h2[0][:, s], h2[1][:, s])
                        if s + 1 < S:
                            stats(LN_B[nxt + 1])
                    dve.wait_ge(rows_in[R_D[blk] % 2], 16 * (R_D[blk] // 2 + 1))
                    with steps.loop(0, A // 2, 2) as i:
                        for par in range(2):
                            down_out(g, s, 2 * i + par, b, par)

        @block.tensor
        def _(pe):
            def transpose_x(m, a_blocks):
                pe.wait_ge(xn_ready, m + 1)
                for k in range(K):
                    if k < 2:
                        reach(pe, h32_ready, K * m)
                        reach(pe, x2_ready, K * a_blocks)
                    else:
                        pe.wait_ge(h32_ready, K * m + k - 1)
                    for a in range(A):
                        ins = nc.tensor.transpose(bank(TB[k % 2])[:, a * P:(a + 1) * P],
                                                  xa[:, a, k * P:(k + 1) * P], ident[:])
                    ins.then_inc(xt_ready, 1)

            def project(n, m, y_before):
                pe.wait_ge(lo_ready, K * (m + 1))
                reach(pe, o_ready, y_before)
                for a in range(A):
                    reach(pe, q_taken, A * n + max(a - 1, 0))
                    for k in range(K):
                        for i, (wp, hp) in enumerate(SPLIT):
                            ins = nc.tensor.matmul(bank(QY[a % 2]), hq[hp][:, k, a * P:(a + 1) * P], WQ[wp][:, k],
                                                   start=(k == 0 and i == 0), stop=(k == K - 1 and i == 2))
                    ins.then_inc(q_ready, 1)

            def transpose_g(n, m):
                pe.wait_ge(g_ready, n + 1)
                pe.wait_ge(h32_ready, K * (m + 1))
                for k in range(K):
                    if k >= 2:
                        pe.wait_ge(x2_ready, K * n + k - 1)
                    for a in range(A):
                        ins = nc.tensor.transpose(bank(TB[k % 2])[:, a * P:(a + 1) * P],
                                                  H[:, a, k * P:(k + 1) * P], ident[:])
                    ins.then_inc(gt_ready, 1)

            def gate_up(g, j, s):
                u = (g * J + j) * S + s
                reach(pe, hd_ready, u - 1 if g or s else u)
                for t in range(2):
                    for k in range(K):
                        for i, (wp, hp) in enumerate(SPLIT):
                            at = (2 * j + t) * BLK + k * P
                            ins = nc.tensor.matmul(bank(GU[2 * s + t]), W[wp][:, bass.ds(at, P)], h2[hp][:, s, k],
                                                   start=(k == 0 and i == 0), stop=(k == K - 1 and i == 2))
                ins.then_inc(gu_ready, 1)

            def down(g, s, q, par):
                d = (g * S + s) * A + q
                reach(pe, o_ready, d - 1 if g or s or par else d)
                for j in range(J):
                    for i, (wp, hp) in enumerate(SPLIT):
                        at = (j * S + s) * BLK + q * P
                        w_at = (2 * J + j) * BLK
                        ins = nc.tensor.matmul(bank(QY[par]), hid[hp][:, bass.ds(at, P)], W[wp][:, w_at:w_at + BLK],
                                               start=(j == 0 and i == 0), stop=(j == J - 1 and i == 2))
                ins.then_inc(y_ready, 1)

            def mod_vec(sections, slot):
                for s in sections:
                    pe.wait_ge(mod_in[s], 16)
                    for kb in range(K):
                        at = (slot(s) * K + kb) * BATCH
                        for k in range(K):
                            ins = nc.tensor.matmul(bank(QY[1])[:, at:at + BATCH], mod_w[:, s, k, kb * P:(kb + 1) * P],
                                                   cT[:, k], start=k == 0, stop=k == K - 1)
                ins.then_inc(vec_mm, 1)

            def mod_row(s, first):
                pe.wait_ge(mod_in[s], 16)
                for b in range(BATCH):
                    for k in range(K):
                        ins = nc.tensor.matmul(bank(GU[first + b]), cT[:, k, b:b + 1].broadcast_to((P, P)),
                                               mod_w[:, s, k], start=k == 0, stop=k == K - 1)
                    ins.then_inc(row_mm, 1)

            pe.wait_ge(silu_c, 1)
            pe.wait_ge(id_ready, 1)
            mod_vec((SA, CA, GA), lambda s: s)
            mod_row(GA, 0)

            pe.wait_ge(wq_ready, 1)
            with pe.Fori(0, NB) as q:
                transpose_x(q, q)
                project(q, q, 0)
                transpose_g(q, q)
            pe.wait_ge(q_taken, A * NB)
            mod_vec((SB, CB), lambda s: s)
            mod_row(GB, 2)
            pe.wait_ge(vec_ready, 2)
            transpose_x(LN_B[0], NB)
            transpose_x(LN_B[1], NB)

            for g in range(G):
                if g == 0:
                    pe.wait_ge(lo_ready, K * (LN_B[1] + 1))
                    with pe.Fori(0, J) as j:
                        pe.wait_ge(w_built, 3 * j + 2)
                        for s in range(S):
                            gate_up(g, j, s)
                    pe.wait_ge(w_built, 3 * J + 1)
                if g == 1:
                    pe.wait_ge(lo_ready, K * (LN_B[S * g + 1] + 1))
                    with pe.Fori(0, NB) as q:
                        n, m = NB + q, LN_A[NB] + q
                        gate_up(g, 2 * q, 0)
                        transpose_x(m, n)
                        gate_up(g, 2 * q, 1)
                        project(n, m, A * S * g)
                        gate_up(g, 2 * q + 1, 0)
                        gate_up(g, 2 * q + 1, 1)
                        transpose_g(n, m)
                if g > 0:
                    pe.wait_ge(lo_ready, K * (LN_B[S * g + 1] + 1))
                    with pe.Fori(2 * NB if g == 1 else 0, J) as j:
                        for s in range(S):
                            gate_up(g, j, s)
                pe.wait_ge(hid_ready, (g + 1) * J * S)
                for s in range(S):
                    nxt = (g + 1) * S + s
                    if g + 1 < G:
                        transpose_x(LN_B[nxt], NB if g < 1 else 2 * NB)
                    with pe.Fori(0, A // 2) as i:
                        down(g, s, 2 * i, 0)
                        down(g, s, 2 * i + 1, 1)


_INS = {"x": "L0_attn_X", "wq": "L0_attn_W_Q", "hh_b": "L0_attn_hh_b", "lut": "L0_ffn_lut", "wmod": "L0_wmod"}


def chunks(gate_idx, up_idx, down_idx):
    def padded(a):
        return np.concatenate([a, np.zeros((J * P - F,) + a.shape[1:], a.dtype)])

    def by_channel(a):
        return padded(a).reshape(J, P, K, P).transpose(0, 3, 2, 1)

    down = padded(np.ascontiguousarray(down_idx.T)).reshape(J, P, K, P)
    parts = [by_channel(gate_idx), by_channel(up_idx), down]
    order = np.stack([a.reshape(J, P, BLK) for a in parts], axis=1).reshape(3 * J, P, BLK)
    return np.concatenate([order, np.zeros((1, P, BLK), order.dtype)])


def rope_tables():
    e = (np.arange(0, ROPE, 2, dtype=np.float32) / np.float32(ROPE)).astype(np.float64)
    inv_freq = (1 / (np.float64(10000) ** e).astype(np.float32)).astype(np.float32)
    angle = np.arange(T, dtype=np.float32)[:, None] * inv_freq[None, :]
    lay = lambda a: np.ascontiguousarray(
        a.astype(np.float32).reshape(T // P, P, ROPE // 2).transpose(1, 0, 2).reshape(P, -1))
    return lay(np.cos(angle.astype(np.float64))), lay(np.sin(angle.astype(np.float64)))


def kernel(**inputs):
    import concourse.bacc as bacc
    from concourse.bass_utils import run_bass_kernel_spmd as run

    nc = bacc.Bacc("TRN2", target_bir_lowering=False, num_devices=1)
    a = {k: np.ascontiguousarray(inputs[v]) for k, v in _INS.items()}
    by_part = lambda v: np.ascontiguousarray(np.asarray(v).reshape(-1, P).T)
    a["gn_w"], a["gn_b"] = by_part(inputs["L0_attn_gn_weight"]), by_part(inputs["L0_attn_gn_bias"])
    a["c_t"] = np.ascontiguousarray(np.asarray(inputs["L0_c"]).reshape(BATCH, K, P).transpose(2, 1, 0))
    a["idx"] = chunks(*(np.asarray(inputs[f"L0_ffn_{n}_idx"]) for n in ("gate", "up", "down")))
    a["cos"], a["sin"] = rope_tables()
    aps = {k: nc.dram_tensor(f"{k}_dram", v.shape, mybir.dt.from_np(v.dtype), kind="ExternalInput").ap()
           for k, v in a.items()}
    out = nc.dram_tensor("out_dram", (BATCH, T, C), F32, kind="ExternalOutput").ap()
    build(nc, **aps, out=out)
    r = run(nc, [{f"{k}_dram": v for k, v in a.items()}], core_ids=[0])
    return r.results[0]["out_dram"]
```

```python
from contextlib import ExitStack, contextmanager

import numpy as np

import concourse.bass as bass
from concourse import mybir

F32 = mybir.dt.float32
F16 = mybir.dt.float16
I32 = mybir.dt.int32
ALU = mybir.AluOpType
ACT = mybir.ActivationFunctionType
AX = mybir.AxisListType.X
RMAX = bass.bass_isa.ReduceOp.max

P = 128
BATCH, T, C = 2, 2048, 512
BLK = 512
A = BLK // P
K = C // P
NB = T // BLK
F = 1376
J = -(-F // P)
F_LAST = F - (J - 1) * P
GRP, GSZ = 32, 16
ROPE = 64
S = 2
G = BATCH * NB // S
LUT = 16
EPS = 1e-5
RSQRT_SEED = float(0x5F3759DF)
EXP1 = float(1 << 23)
SA, CA, GA, SB, CB, GB = range(6)
NCH = 3 * J
AHEAD = 4
SPLIT = ((0, 0), (0, 1), (1, 0))


class Steps:

    def __init__(self, eng, sem):
        self.eng, self.sem, self.base, self.n = eng, sem, 0, 0

    def step(self, ins):
        ins.then_inc(self.sem, 1)
        self.n += 1
        self.eng.wait_ge(self.sem, self.base + self.n)

    @contextmanager
    def loop(self, first, end, per):
        start = self.base + self.n
        with self.eng.Fori(first, end) as i:
            self.base, self.n = start + (i - first) * per, 0
            yield i
            assert self.n == per, self.n
        self.base, self.n = start + (end - first) * per, 0


def reach(eng, sem, value):
    if not isinstance(value, int) or value > 0:
        eng.wait_ge(sem, value)


def build(nc, x, wq, hh_b, gn_w, gn_b, lut, idx, c_t, wmod, cos, sin, out):
    x2_dram = nc.dram_tensor("x2_dram", (BATCH, NB, P, A * C), F32, kind="Internal").ap()
    x_rows = x.rearrange("b (m p q) n -> b m p q n", p=P, q=A)
    x_toks = x.rearrange("b (m a p) n -> b m p a n", p=P, a=A)
    x2_rows = x2_dram.rearrange("b m p (q n) -> b m p q n", q=A)
    out_rows = out.rearrange("b (m p q) n -> b m p q n", p=P, q=A)

    with ExitStack() as ctx:
        def sb(name, shape, dt):
            return ctx.enter_context(nc.sbuf_tensor(name, shape, dt))

        def sem(name):
            return ctx.enter_context(nc.semaphore(name))

        w_all = sb("w_all", [P, 2 * 3 * J * BLK], F16)
        W = [w_all[:, h * 3 * J * BLK:(h + 1) * 3 * J * BLK] for h in range(2)]
        MOD_AT = (0, 8, 16, 24, NCH + 16, NCH + 24)
        mod_w = [w_all[:, at * BLK:at * BLK + 2 * K * C].bitcast(F32).rearrange("p (k n) -> p k n", k=K)
                 for at in MOD_AT]
        hid = [sb(f"hid{h}", [P, J * S * BLK], F16) for h in range(2)]
        h2 = [sb(f"h2_{h}", [P, S, K, BLK], F16) for h in range(2)]
        work = sb("work", [P, 2 * A * C], F32)
        H = work[:, 0:A * C].rearrange("p (a n) -> p a n", a=A)
        hq_all = work[:, A * C:2 * A * C].bitcast(F16)
        hq = [hq_all[:, h * K * BLK:(h + 1) * K * BLK].rearrange("p (k n) -> p k n", k=K) for h in range(2)]
        R = [sb(f"R{i}", [P, A * C], F32) for i in range(2)]
        xa = sb("xa", [P, A, C], F32)
        h32 = sb("h32", [P, 2, BLK], F32)
        sq = sb("sq", [P, 2, BLK], F32)
        WQ = [sb(f"WQ{h}", [P, K, C], F16) for h in range(2)]
        cosT = sb("cosT", [P, T // P * (ROPE // 2)], F32)
        sinT = sb("sinT", [P, T // P * (ROPE // 2)], F32)
        hhS = sb("hhS", [P, C], F32)
        gaB = sb("gaB", [P, BATCH, C], F32)
        gbB = sb("gbB", [P, BATCH, C], F32)
        sg = sb("sg", [P, S, BLK], F32)
        ident = sb("ident", [P, P], F32)
        vec = sb("vec", [P, 5, K, BATCH], F32)
        gnw = sb("gnw", [P, K], F32)
        gnb = sb("gnb", [P, K], F32)
        cT = sb("cT", [P, K, BATCH], F32)
        lutS = sb("lutS", [P, LUT], F32)
        lutD = sb("lutD", [P, LUT // 2], F32)
        st = sb("st", [P, A, 6], F32)
        mv = sb("mv", [P, A, 2], F32)
        ls = sb("ls", [P, 5, A], F32)
        gs = sb("gs", [P, 4, A * GRP], F32)
        col = sb("col", [P, 16], F32)
        hd = sb("hd", [P, S, BLK], F32)
        ps = ctx.enter_context(nc.psum_tensor("ps", [P, 8 * BLK], F32))

        def bank(i):
            return ps[:, i * BLK:(i + 1) * BLK]

        GU, TB, QY = (0, 1, 2, 3), (4, 5), (6, 7)
        h2_flat = [h.rearrange("p s k n -> p (s k n)").bitcast(F32) for h in h2]

        def part(t, i):
            return t[:, i * BLK:(i + 1) * BLK]

        class Scratch:
            def __init__(self, idx, bit, mask, pairs):
                self.idx, self.bit = [i.bitcast(I32) for i in idx], [b.bitcast(I32) for b in bit]
                self.mask, self.pairs = [m.bitcast(I32) for m in mask], pairs

        in_attn = Scratch([part(h2_flat[0], i) for i in (0, 1)], [part(h2_flat[0], i) for i in (2, 3)],
                          [part(h2_flat[1], i) for i in (0, 1, 2)],
                          [[part(hid[i][:, :].bitcast(F32), g) for g in range(8)] for i in range(2)])
        in_ffn = Scratch([h32[:, i] for i in range(2)], [sq[:, i] for i in range(2)], [xa[:, i] for i in range(3)],
                         [[part(work, g) for g in range(8)], [part(R[g // 4], g % 4) for g in range(8)]])

        def scratch(early):
            return in_attn if early else in_ffn

        (c_wqmax, c_wqall, c_sq, c_isq, c_s, c_is, c_sh, c_kappa, c_kappa2, c_e, c_tmp) = \
            (col[:, i:i + 1] for i in range(11))

        x_in = sem("x_in"); x_in_h = sem("x_in_h"); rows_in = [sem("rows_in0"), sem("rows_in1")]
        wq_in = sem("wq_in"); const_in = sem("const_in"); rope_in = sem("rope_in")
        mod_in = [sem(f"mod_in{s}") for s in range(6)]
        idx_in = [sem("idx_in0"), sem("idx_in1")]
        x2_out = sem("x2_out"); y_out = [sem("y_out0"), sem("y_out1")]
        id_zero = sem("id_zero"); id_ready = sem("id_ready"); wq_all = sem("wq_all")
        dstep = sem("dstep")
        silu_c = sem("silu_c"); vec_mm = sem("vec_mm"); row_mm = sem("row_mm")
        vec_ready = sem("vec_ready"); row_ready = sem("row_ready")
        wq_max = sem("wq_max"); wq_ready = sem("wq_ready"); scales_ready = sem("scales_ready")
        ln_stats = sem("ln_stats"); xn_ready = sem("xn_ready"); xt_ready = sem("xt_ready")
        h32_ready = sem("h32_ready"); hi_ready = sem("hi_ready"); lo_ready = sem("lo_ready")
        q_ready = sem("q_ready"); q_taken = sem("q_taken"); pre_tanh = sem("pre_tanh"); tanh_ready = sem("tanh_ready")
        centered = sem("centered"); squared = sem("squared"); sq_summed = sem("sq_summed")
        g_ready = sem("g_ready"); gt_ready = sem("gt_ready"); x2_ready = sem("x2_ready")
        idx_used = sem("idx_used"); bit_ready = sem("bit_ready"); w_hi = sem("w_hi"); pairs_ready = sem("pairs_ready"); w_built = sem("w_built")
        gu_ready = sem("gu_ready"); silu_ready = sem("silu_ready"); hd_ready = sem("hd_ready")
        hid_hi_ready = sem("hid_hi_ready"); hid_ready = sem("hid_ready")
        y_ready = sem("y_ready"); o_ready = sem("o_ready")

        block = ctx.enter_context(nc.Block())

        LN_A = [0, 1, 2, 3, 8, 9, 10, 11]
        LN_B = [4, 5, 6, 7, 12, 13, 14, 15]
        R_A = [0, 1, 2, 3, 6, 7, 8, 9]
        R_D = [4, 5, 10, 11, 12, 13, 14, 15]

        @block.sync
        def _(sp):
            def load_x(src, m, tile=xa):
                reach(sp, xt_ready, K * m if tile is xa else 0)
                sp.dma_start(tile[:], src).then_inc(x_in if tile is xa else x_in_h, 16)

            def load_idx(w, par, early):
                reach(sp, idx_used, w - 1)
                sp.dma_start(scratch(early).idx[par], idx[w] if isinstance(w, int) else
                             idx[bass.ds(w, 1)].squeeze(0)).then_inc(idx_in[par], 16)

            def load_rows(r, src):
                sp.dma_start(R[r].rearrange("p (q n) -> p q n", q=A), src).then_inc(rows_in[r], 16)

            def rows_of_block(b, q):
                return x.rearrange("b (m p q) n -> b q p m n", p=P, q=A)[b, q]

            def x2_of_block(b, q):
                return x2_dram.rearrange("b m p (q n) -> b q p m n", q=A)[b, q]

            sp.dma_start(cT[:], c_t).then_inc(const_in, 16)
            sp.dma_start(lutS[:], lut.partition_broadcast(P)).then_inc(const_in, 16)
            sp.dma_start(hhS[:], hh_b.partition_broadcast(P)).then_inc(const_in, 16)
            sp.dma_start(gnw[:], gn_w).then_inc(const_in, 16)
            sp.dma_start(gnb[:], gn_b).then_inc(const_in, 16)
            load_x(x_toks[0, 0], 0)
            wq_f32 = hid[0][:, 0:2 * K * C].bitcast(F32).rearrange("p (k n) -> p k n", k=K)
            sp.dma_start(wq_f32, wq.rearrange("(k p) n -> p k n", p=P)).then_inc(wq_in, 16)
            mod_v = wmod.rearrange("(k p) (s n) -> s p k n", p=P, s=6)
            for s in (SA, CA, GA):
                sp.dma_start(mod_w[s], mod_v[s]).then_inc(mod_in[s], 16)
            sp.dma_start(cosT[:], cos).then_inc(rope_in, 16)
            sp.dma_start(sinT[:], sin).then_inc(rope_in, 16)
            load_rows(0, rows_of_block(0, 0))
            for s in (SB, CB, GB):
                sp.dma_start(mod_w[s], mod_v[s]).then_inc(mod_in[s], 16)

            load_idx(0, 0, True)
            load_idx(1, 1, True)

            for q in range(NB):
                if q + 1 < NB:
                    load_x(x_toks[0, q + 1], q + 1)
                    reach(sp, x2_out, 16 * q)
                    load_rows((q + 1) % 2, rows_of_block(0, q + 1))
                for i in range(2, AHEAD + 2):
                    if i == AHEAD + 1:
                        sp.wait_ge(x2_ready, K * (q + 1))
                        sp.dma_start(x2_of_block(0, q), R[q % 2].rearrange("p (q n) -> p q n", q=A)) \
                          .then_inc(x2_out, 16)
                    w = AHEAD * q + i
                    if w < AHEAD * NB:
                        load_idx(w, w % 2, True)
            sp.wait_ge(x2_out, 16 * NB)
            load_x(x2_rows[0, 0], LN_B[0])
            load_x(x2_rows[0, 1], LN_B[1], H)
            sp.wait_ge(lo_ready, K * (LN_B[1] + 1))
            for w in (AHEAD * NB, AHEAD * NB + 1):
                load_idx(w, w % 2, False)
            with sp.Fori(AHEAD * NB // 2 + 1, NCH // 2) as i:
                for par in range(2):
                    load_idx(2 * i + par, par, False)
            load_idx(NCH - 1, 0, False)

            def load_ffn_block(blk):
                load_x(x2_rows[blk // NB, blk % NB], LN_B[blk])

            def out_rows_of(g, s, first):
                blk = g * S + s
                with sp.Fori(first, first + A // 2) as q:
                    sp.wait_ge(o_ready, blk * A + q + 1)
                    sp.dma_start(out_rows[blk // NB, blk % NB, :, bass.ds(q, 1), :].squeeze(1),
                                 R[R_D[blk] % 2][:, bass.ds(q * C, C)]).then_inc(y_out[R_D[blk] % 2], 16)

            def down_io(g):
                for s in range(S):
                    out_rows_of(g, s, 0)
                    if g + 1 < G and s == 0:
                        load_ffn_block((g + 1) * S + 1)
                    if g == 0 and s == 1:
                        load_x(x_toks[1, 0], LN_A[NB])
                    if g == 1 and s == 1:
                        load_ffn_block(3 * S)
                    out_rows_of(g, s, A // 2)

            def load_down_rows(g, s):
                blk = g * S + s
                if g >= 2:
                    sp.wait_ge(y_out[R_D[blk] % 2], 16 * A * (blk // 2))
                load_rows(R_D[blk] % 2, x2_rows[blk // NB, blk % NB])

            for g in range(G):
                if g == 0:
                    sp.wait_ge(w_built, NCH)
                    load_ffn_block(S)
                if g == 1:
                    for q in range(NB):
                        n = NB + q
                        if q == 0:
                            sp.wait_ge(y_out[R_A[n] % 2], 16 * A)
                            load_rows(R_A[n] % 2, rows_of_block(1, 0))
                        if q + 1 < NB:
                            load_x(x_toks[1, q + 1], LN_A[n] + 1)
                            if q == 0:
                                sp.wait_ge(y_out[R_A[n + 1] % 2], 16 * A)
                            reach(sp, x2_out, 16 * n)
                            load_rows(R_A[n + 1] % 2, rows_of_block(1, q + 1))
                        sp.wait_ge(x2_ready, K * (n + 1))
                        sp.dma_start(x2_of_block(1, q), R[R_A[n] % 2].rearrange("p (q n) -> p q n", q=A)) \
                          .then_inc(x2_out, 16)
                    sp.wait_ge(x2_out, 16 * BATCH * NB)
                    load_ffn_block(2 * S)
                for s in range(S):
                    load_down_rows(g, s)
                down_io(g)
            for r in range(2):
                sp.wait_ge(y_out[r], 16 * A * BATCH * NB // 2)

        @block.gpsimd
        def _(pool):
            nc.gpsimd.memset(ident[:], 0.0).then_inc(id_zero, 1)
            pool.wait_ge(id_zero, 1)
            nc.gpsimd.affine_select(out=ident[:], in_=ident[:], compare_op=ALU.not_equal, fill=1.0, base=0,
                                    pattern=[[-1, P]], channel_multiplier=1).then_inc(id_ready, 1)
            pool.wait_ge(wq_max, 1)
            nc.gpsimd.partition_all_reduce(c_wqall, c_wqmax, P, RMAX).then_inc(wq_all, 1)

            def split_lo(m, hi, lo):
                for k in range(K):
                    pool.wait_ge(hi_ready, K * m + k + 1)
                    nc.gpsimd.tensor_tensor(lo[:, k], h32[:, k % 2], hi[:, k], ALU.subtract).then_inc(lo_ready, 1)

            def table_lo(w, par, early):
                pool.wait_ge(w_hi, w + 1)
                hi, lo = (W[h][:, bass.ds(w * BLK, BLK)] for h in range(2))
                nc.gpsimd.tensor_tensor(lo, scratch(early).pairs[par][0], hi, ALU.subtract).then_inc(w_built, 1)

            split_lo(0, hq[0], hq[1])
            with pool.Fori(0, NB - 1) as q:
                table_lo(AHEAD * q, 0, True)
                split_lo(q + 1, hq[0], hq[1])
                for i in range(1, AHEAD):
                    table_lo(AHEAD * q + i, i % 2, True)
            for w in range(AHEAD * (NB - 1), AHEAD * NB):
                table_lo(w, w % 2, True)
            for s in range(S):
                split_lo(LN_B[s], h2[0][:, s], h2[1][:, s])
            with pool.Fori(AHEAD * NB // 2, NCH // 2) as i:
                for par in range(2):
                    table_lo(2 * i + par, par, False)
            table_lo(NCH - 1, 0, False)
            for g in range(G):
                if g == 1:
                    split_lo(LN_A[NB], hq[0], hq[1])
                    with pool.Fori(LN_A[NB] + 1, LN_A[2 * NB - 1] + 1) as m:
                        split_lo(m, hq[0], hq[1])
                if g + 1 < G:
                    for s in range(S):
                        split_lo(LN_B[(g + 1) * S + s], h2[0][:, s], h2[1][:, s])

        @block.scalar
        def _(act):
            def norm(m, x_=xa):
                act.wait_ge(ln_stats, m + 1)
                for a in range(A):
                    ins = nc.scalar.activation(x_[:, a], x_[:, a], ACT.Identity,
                                               bias=ls[:, 3, a:a + 1], scale=ls[:, 2, a:a + 1])
                ins.then_inc(xn_ready, 1)

            def affine(m, scale, shift, b, dest, dest_free):
                for k in range(K):
                    act.wait_ge(xt_ready, K * m + k + 1)
                    reach(act, lo_ready, K * m + max(k - 1, 0))
                    nc.scalar.activation(h32[:, k % 2], bank(TB[k % 2]), ACT.Identity,
                                         bias=vec[:, shift, k, b:b + 1], scale=vec[:, scale, k, b:b + 1]) \
                      .then_inc(h32_ready, 1)
                    act.wait_ge(h32_ready, K * m + k + 1)
                    if k == 0:
                        dest_free()
                    nc.scalar.activation(dest[:, k], h32[:, k % 2], ACT.Copy).then_inc(hi_ready, 1)

            def tanh(n, a):
                act.wait_ge(pre_tanh, A * n + a + 1)
                nc.scalar.activation(H[:, a], H[:, a], ACT.Tanh, scale=c_isq).then_inc(tanh_ready, 1)

            def square(n, a):
                act.wait_ge(centered, A * n + a + 1)
                reach(act, sq_summed, A * n + max(a - 1, 0))
                nc.scalar.activation(sq[:, a % 2], H[:, a], ACT.Square).then_inc(squared, 1)

            def silu(g, j, s):
                u = (g * J + j) * S + s
                act.wait_ge(gu_ready, u + 1)
                reach(act, hd_ready, u - 1)
                nc.scalar.activation(sg[:, s], bank(GU[2 * s]), ACT.Silu, scale=c_is).then_inc(silu_ready, 1)

            def hid_hi(g, j, s):
                u = (g * J + j) * S + s
                act.wait_ge(hd_ready, u + 1)
                nc.scalar.activation(hid[0][:, bass.ds((j * S + s) * BLK, BLK)], hd[:, s], ACT.Copy) \
                  .then_inc(hid_hi_ready, 1)

            def pair_tables(w, par, early):
                act.wait_ge(bit_ready, w + 1)
                reach(act, w_built, w - 1)
                s_ = scratch(early)
                for g in range(8):
                    ins = nc.scalar.activation(s_.pairs[par][g], s_.bit[par], ACT.Identity,
                                               bias=lutS[:, 2 * g:2 * g + 1], scale=lutD[:, g:g + 1])
                ins.then_inc(pairs_ready, 1)

            def tanh_squares(n):
                tanh(n, 0); tanh(n, 1); square(n, 0); tanh(n, 2)
                square(n, 1); tanh(n, 3); square(n, 2); square(n, 3)

            act.wait_ge(const_in, 80)
            nc.scalar.activation(cT[:], cT[:], ACT.Silu).then_inc(silu_c, 1)

            act.wait_ge(vec_ready, 1)
            norm(0)
            affine(0, CA, SA, 0, hq[0], lambda: None)
            pair_tables(0, 0, True)
            with act.Fori(0, NB - 1) as q:
                norm(q + 1)
                pair_tables(AHEAD * q + 1, 1, True)
                tanh_squares(q)
                affine(q + 1, CA, SA, 0, hq[0], lambda: act.wait_ge(q_ready, A * q + A))
                for i in range(2, AHEAD + 1):
                    pair_tables(AHEAD * q + i, i % 2, True)
            w = AHEAD * (NB - 1)
            pair_tables(w + 1, 1, True)
            tanh_squares(NB - 1)
            for i in range(2, AHEAD):
                pair_tables(w + i, i % 2, True)

            act.wait_ge(vec_ready, 2)
            act.wait_ge(w_built, AHEAD * NB)
            for s in range(S):
                norm(LN_B[s], H if s else xa)
                affine(LN_B[s], CB, SB, 0, h2[0][:, s], lambda: None)

            first = AHEAD * NB
            pair_tables(first, 0, False)

            def tables_units(j):
                for s in range(S):
                    silu(0, j, s)
                    pair_tables(first + 2 * j + s + 1, (s + 1) % 2, False)
                    hid_hi(0, j, s)

            tables_units(0)
            with act.Fori(1, (NCH - 1 - first) // 2) as j:
                tables_units(j)
            with act.Fori((NCH - 1 - first) // 2, J) as j:
                for s in range(S):
                    silu(0, j, s)
                    hid_hi(0, j, s)

            def gate_units(g, first, end):
                with act.Fori(first, end) as j:
                    for s in range(S):
                        silu(g, j, s)
                        hid_hi(g, j, s)

            for g in range(G):
                if g == 1:
                    norm(LN_A[NB])
                    gate_units(g, 0, 1)
                    affine(LN_A[NB], CA, SA, 1, hq[0], lambda: None)
                    gate_units(g, 1, 2)

                    def attn_unit(q, i):
                        j = 2 + 2 * q + i // S
                        silu(g, j, i % S)
                        hid_hi(g, j, i % S)

                    with act.Fori(0, NB - 1) as q:
                        n, m = NB + q, LN_A[NB] + q
                        norm(m + 1)
                        tanh_squares(n)
                        attn_unit(q, 0)
                        affine(m + 1, CA, SA, 1, hq[0], lambda: act.wait_ge(q_ready, A * n + A))
                        for i in range(1, 2 * S):
                            attn_unit(q, i)
                    tanh_squares(2 * NB - 1)
                    for i in range(2 * S):
                        attn_unit(NB - 1, i)
                    gate_units(g, 2 + 2 * NB, J)
                if g > 1:
                    gate_units(g, 0, J)
                if g + 1 < G:
                    for s in range(S):
                        blk = (g + 1) * S + s
                        norm(LN_B[blk])
                        affine(LN_B[blk], CB, SB, blk // NB, h2[0][:, s], lambda: None)

        @block.vector
        def _(dve):
            steps = Steps(dve, dstep)
            step = steps.step
            v = nc.vector

            def alone():
                v.memset(col[:, 15:16], 0.0)

            def rsqrt(x_, t_, y_):
                step(v.tensor_scalar(t_.bitcast(I32), x_.bitcast(I32), 1, None, ALU.logical_shift_right))
                step(v.tensor_scalar(y_.bitcast(I32), t_.bitcast(I32), -1.0, RSQRT_SEED, ALU.mult, ALU.add))
                for _ in range(3):
                    step(v.tensor_tensor(t_, y_, y_, ALU.mult))
                    step(v.scalar_tensor_tensor(t_, t_, -0.5, x_, ALU.mult, ALU.mult))
                    step(v.scalar_tensor_tensor(y_, t_, 1.5, y_, ALU.add, ALU.mult))

            def stats(m, x_=xa):
                if x_ is xa:
                    late = not isinstance(m, int) or m > LN_B[1]
                    dve.wait_ge(x_in, 16 * m + (0 if late else 16))
                else:
                    dve.wait_ge(x_in_h, 16)
                for a in range(A):
                    ins = v.bn_stats(st[:, a], x_[:, a])
                step(ins)
                alone()
                for a in range(A):
                    ins = v.bn_aggr(mv[:, a], st[:, a])
                step(ins)
                reach(dve, xn_ready, m)
                step(v.tensor_scalar(ls[:, 0], mv[:, :, 1], EPS, None, ALU.add))
                rsqrt(ls[:, 0], ls[:, 1], ls[:, 2])
                v.scalar_tensor_tensor(ls[:, 3], mv[:, :, 0], -1.0, ls[:, 2], ALU.mult, ALU.mult) \
                 .then_inc(ln_stats, 1)

            def rope_relu(n, q, a):
                reach(dve, pre_tanh, A * n + a)
                dve.wait_ge(q_ready, A * n + a + 1)
                Q = bank(QY[a % 2])
                half = ROPE // 2
                at = (q * A + a) * half
                cs, sn = cosT[:, bass.ds(at, half)], sinT[:, bass.ds(at, half)]
                Qr = Q[:, 0:ROPE].rearrange("p (i e) -> p e i", e=2)
                rot2 = gs2[:, 0:ROPE].rearrange("p (i e) -> p e i", e=2)
                tmp2 = gs2[:, ROPE:2 * ROPE].rearrange("p (i e) -> p e i", e=2)
                for e in range(2):
                    v.tensor_tensor(rot2[:, e], Qr[:, e], cs, ALU.mult)
                v.tensor_tensor(tmp2[:, 0], Qr[:, 1], sn, ALU.mult)
                step(v.tensor_tensor(tmp2[:, 1], Qr[:, 0], sn, ALU.mult))
                v.tensor_tensor(rot2[:, 0], rot2[:, 0], tmp2[:, 0], ALU.subtract)
                step(v.tensor_tensor(rot2[:, 1], rot2[:, 1], tmp2[:, 1], ALU.add))
                v.scalar_tensor_tensor(H[:, a, ROPE:], Q[:, ROPE:], 0.0, hhS[:, ROPE:], ALU.max, ALU.add) \
                 .then_inc(q_taken, 1)
                v.scalar_tensor_tensor(H[:, a, 0:ROPE], gs2[:, 0:ROPE], 0.0, hhS[:, 0:ROPE],
                                       ALU.max, ALU.add).then_inc(pre_tanh, 1)

            def center(n, a):
                dve.wait_ge(tanh_ready, A * n + a + 1)
                Hg = H[:, a].rearrange("p (g e) -> p g e", e=GSZ)
                sums = gs[:, 0, a * GRP:(a + 1) * GRP]
                step(v.tensor_reduce(sums, Hg, axis=AX, op=ALU.add))
                step(v.tensor_scalar(sums, sums, 1.0 / GSZ, None, ALU.mult))
                v.tensor_tensor(Hg, Hg, sums.unsqueeze(2).broadcast_to((P, GRP, GSZ)), ALU.subtract) \
                 .then_inc(centered, 1)

            def sum_squares(n, a):
                dve.wait_ge(squared, A * n + a + 1)
                v.tensor_reduce(gs[:, 1, a * GRP:(a + 1) * GRP], sq[:, a % 2].rearrange("p (g e) -> p g e", e=GSZ),
                                axis=AX, op=ALU.add).then_inc(sq_summed, 1)

            def group_scale(n, b):
                dve.wait_ge(sq_summed, A * n + A)
                step(v.tensor_scalar(gs[:, 1], gs[:, 1], 1.0 / GSZ, EPS, ALU.mult, ALU.add))
                rsqrt(gs[:, 1], gs[:, 2], gs[:, 3])
                r = gs[:, 3].rearrange("p (a g) -> p a g", a=A)
                ga = vec[:, GA, :, b].unsqueeze(2).broadcast_to((P, A, GRP))
                step(v.tensor_tensor(r, r, ga, ALU.mult))
                Hg = H.rearrange("p a (g e) -> p (a g) e", e=GSZ)
                v.tensor_tensor(Hg, Hg, gs[:, 3].unsqueeze(2).broadcast_to((P, A * GRP, GSZ)), ALU.mult) \
                 .then_inc(g_ready, 1)

            def rows_ready(n, b, r, loads):
                dve.wait_ge(rows_in[r], 16 * loads)
                for k in range(K):
                    Rk = R[r][:, k * C:(k + 1) * C]
                    ins = v.scalar_tensor_tensor(Rk, gaB[:, b], gnb[:, k:k + 1], Rk, ALU.mult, ALU.add)
                step(ins)

            def residual(n, r):
                for k in range(K):
                    Rk = R[r][:, k * C:(k + 1) * C]
                    dve.wait_ge(gt_ready, K * n + k + 1)
                    v.scalar_tensor_tensor(Rk, bank(TB[k % 2]), gnw[:, k:k + 1], Rk, ALU.mult, ALU.add) \
                     .then_inc(x2_ready, 1)

            def group_norm(n, q):
                rope_relu(n, q, 0); rope_relu(n, q, 1); center(n, 0); rope_relu(n, q, 2)
                center(n, 1); sum_squares(n, 0); rope_relu(n, q, 3); center(n, 2)
                sum_squares(n, 1); center(n, 3); sum_squares(n, 2); sum_squares(n, 3)

            def low_bit(w, par, early):
                dve.wait_ge(idx_in[par], 16 * ((w - par) // 2 + 1) if isinstance(w, int) else 8 * (w - par) + 16)
                s_ = scratch(early)
                v.tensor_scalar(s_.bit[par], s_.idx[par], 1, None, ALU.bitwise_and).then_inc(bit_ready, 1)

            def build_chunk(w, par, early, more=True):
                s_ = scratch(early)
                for i in range(3):
                    ins = v.tensor_scalar(s_.mask[i], s_.idx[par], 2 << i, None, ALU.bitwise_and)
                ins.then_inc(idx_used, 1)
                if more:
                    low_bit(w + 1, 1 - par, early)
                dve.wait_ge(idx_used, w + 1)
                dve.wait_ge(pairs_ready, w + 1)
                g = s_.pairs[par]
                for level, span in ((0, 1), (1, 2), (2, 4)):
                    alone()
                    for at in range(0, 8, 2 * span):
                        ins = v.copy_predicated(g[at], s_.mask[level], g[at + span])
                    step(ins)
                v.tensor_scalar(W[0][:, bass.ds(w * BLK, BLK)], g[0], 1.0, None, ALU.mult).then_inc(w_hi, 1)

            def hidden(g, j, s):
                u = (g * J + j) * S + s
                reach(dve, hid_ready, u - 1)
                dve.wait_ge(silu_ready, u + 1)
                v.scalar_tensor_tensor(hd[:, s], bank(GU[2 * s + 1]), c_kappa, sg[:, s], ALU.mult, ALU.mult) \
                 .then_inc(hd_ready, 1)

            def hid_lo(g, j, s):
                u = (g * J + j) * S + s
                dve.wait_ge(hid_hi_ready, u + 1)
                at = bass.ds((j * S + s) * BLK, BLK)
                v.tensor_tensor(hid[1][:, at], hd[:, s], hid[0][:, at], ALU.subtract).then_inc(hid_ready, 1)

            def down_out(g, s, q, b, par):
                d = (g * S + s) * A + q
                r = R_D[g * S + s] % 2
                dve.wait_ge(y_ready, d + 1)
                step(v.scalar_tensor_tensor(hd[:, par], bank(QY[par]), c_kappa2, gbB[:, b], ALU.mult, ALU.mult))
                Rq = R[r][:, bass.ds(q * C, C)]
                v.tensor_tensor(Rq, hd[:, par], Rq, ALU.add).then_inc(o_ready, 1)

            dve.wait_ge(const_in, 80)
            gs2 = gs[:, 2]

            def magnitude(dst, src):
                step(v.tensor_scalar(dst.bitcast(I32), src.bitcast(I32), 0x7FFFFFFF, None, ALU.bitwise_and))

            def exponent(dst, src, lowest, highest):
                step(v.tensor_scalar(dst.bitcast(I32), src.bitcast(I32), 0x7F800000, None, ALU.bitwise_and))
                step(v.tensor_scalar(dst.bitcast(I32), dst.bitcast(I32), lowest * EXP1, highest * EXP1,
                                     ALU.max, ALU.min))

            def field(dst, src, times, plus):
                step(v.tensor_scalar(dst.bitcast(I32), src.bitcast(I32), float(times), plus * EXP1,
                                     ALU.mult, ALU.add))

            tmp16 = gs[:, 0, 0:LUT]
            magnitude(tmp16, lutS[:])
            step(v.tensor_reduce(c_tmp, tmp16, axis=AX, op=ALU.max))
            exponent(c_e, c_tmp, 60, 186)
            field(c_s, c_e, -1, 264)
            field(c_is, c_s, -1, 254)
            field(c_sh, c_e, -2, 374)
            field(c_tmp, c_sh, -1, 254)
            step(v.tensor_tensor(c_kappa, c_is, c_sh, ALU.mult))
            step(v.tensor_tensor(c_kappa2, c_is, c_tmp, ALU.mult))
            step(v.tensor_scalar(lutS[:], lutS[:], c_s, None, ALU.mult))
            lp = lutS.rearrange("p (g e) -> p e g", e=2)
            v.tensor_tensor(lutD[:], lp[:, 1], lp[:, 0], ALU.subtract)

            wq_f32 = hid[0][:, 0:2 * K * C].bitcast(F32)
            wq_s = hid[1][:, 0:2 * K * C].bitcast(F32)
            dve.wait_ge(wq_in, 16)
            magnitude(wq_s, wq_f32)
            v.tensor_reduce(c_wqmax, wq_s, axis=AX, op=ALU.max).then_inc(wq_max, 1)
            stats(0)
            dve.wait_ge(wq_all, 1)
            exponent(c_e, c_wqall, 60, 186)
            field(c_sq, c_e, -1, 264)
            field(c_isq, c_sq, -1, 254)
            v.tensor_scalar(hhS[:], hhS[:], c_sq, None, ALU.mult)
            step(v.tensor_scalar(wq_s, wq_f32, c_sq, None, ALU.mult))
            step(v.tensor_scalar(WQ[0].rearrange("p k n -> p (k n)"), wq_s, 1.0, None, ALU.mult))
            v.tensor_tensor(WQ[1].rearrange("p k n -> p (k n)"), wq_s, WQ[0].rearrange("p k n -> p (k n)"),
                            ALU.subtract).then_inc(wq_ready, 1)

            vps = bank(QY[1])[:, 0:5 * K * BATCH].rearrange("p (s k b) -> p s k b", s=5, k=K)

            def gate_of(dst, src, tmp, tmp2):
                v.tensor_scalar(tmp, src, 0.0, 2.0, ALU.is_ge, ALU.mult)
                magnitude(tmp2, src)
                step(v.tensor_scalar(tmp2, tmp2, 0.25, None, ALU.max))
                return v.scalar_tensor_tensor(dst, tmp, 1.0, tmp2, ALU.subtract, ALU.mult)

            dve.wait_ge(vec_mm, 1)
            v.tensor_copy(vec[:, SA], vps[:, SA])
            v.tensor_scalar(vec[:, CA], vps[:, CA], 1.0, None, ALU.add)
            gv = vps[:, GA].rearrange("p k b -> p (k b)")
            gate_of(vec[:, GA].rearrange("p k b -> p (k b)"), gv, gs[:, 0, 0:K * BATCH], gs[:, 1, 0:K * BATCH]) \
                .then_inc(vec_ready, 1)
            for b in range(BATCH):
                dve.wait_ge(row_mm, b + 1)
                step(gate_of(gaB[:, b], bank(GU[b]), hd[:, 0], hd[:, 1]))
            dve.wait_ge(rope_in, 32)

            low_bit(0, 0, True)

            def attn_block(q, half, last):
                w = AHEAD * q
                if not last:
                    stats(q + 1)
                build_chunk(w, 0, True)
                group_norm(q, q)
                group_scale(q, 0)
                build_chunk(w + 1, 1, True)
                rows_ready(q, 0, half, (q - half) // 2 + 1)
                residual(q, half)
                for i in range(2, AHEAD):
                    build_chunk(w + i, i % 2, True, not last or i + 1 < AHEAD)

            attn_block(0, 0, False)
            attn_block(1, 1, False)
            attn_block(2, 0, False)
            attn_block(3, 1, True)

            dve.wait_ge(vec_mm, 2)
            v.tensor_copy(vec[:, SB], vps[:, SB])
            v.tensor_scalar(vec[:, CB], vps[:, CB], 1.0, None, ALU.add).then_inc(vec_ready, 1)
            for b in range(BATCH):
                dve.wait_ge(row_mm, BATCH + b + 1)
                step(gate_of(gbB[:, b], bank(GU[2 + b]), hd[:, 0], hd[:, 1]))
            stats(LN_B[0])
            stats(LN_B[1], H)

            first = AHEAD * NB
            low_bit(first, 0, False)

            def tables_unit(j, s, lo):
                build_chunk(first + 2 * j + s, s % 2, False)
                hidden(0, j, s)
                if lo:
                    hid_lo(0, j - (1 - s), 1 - s)

            tables_unit(0, 0, False)
            tables_unit(0, 1, True)
            with steps.loop(1, (NCH - 1 - first) // 2, 6) as j:
                for s in range(S):
                    tables_unit(j, s, True)
            build_chunk(NCH - 1, 0, False, False)
            with steps.loop((NCH - 1 - first) // 2, J, 0) as j:
                for s in range(S):
                    hidden(0, j, s)
                    hid_lo(0, j - (1 - s), 1 - s)
            hid_lo(0, J - 1, 1)
            dve.wait_ge(w_built, NCH)
            for h in range(2):
                ins = v.memset(W[h][F_LAST:P, (NCH - 1) * BLK:], 0.0)
            ins.then_inc(w_built, 1)

            def gate_units(g, first, end):
                with steps.loop(first, end, 0) as j:
                    for s in range(S):
                        hidden(g, j, s)
                        hid_lo(g, j, s)

            for g in range(G):
                b = g * S // NB
                if g == 1:
                    stats(LN_A[NB])
                    gate_units(g, 0, 2)

                    def attn_unit(q, i):
                        j = 2 + 2 * q + i // S
                        hidden(g, j, i % S)
                        hid_lo(g, j, i % S)

                    def attn_block(q, half, last):
                        n, m = NB + q, LN_A[NB] + q
                        if not last:
                            stats(m + 1)
                        group_norm(n, q)
                        attn_unit(q, 0)
                        group_scale(n, 1)
                        rows_ready(n, 1, half, (R_A[NB] + q - half) // 2 + 1)
                        attn_unit(q, 1)
                        residual(n, half)
                        attn_unit(q, 2)
                        attn_unit(q, 3)

                    for q in range(NB):
                        attn_block(q, q % 2, q == NB - 1)
                    gate_units(g, 2 + 2 * NB, J)
                if g > 1:
                    gate_units(g, 0, J)
                for s in range(S):
                    blk, nxt = g * S + s, (g + 1) * S + s
                    if g + 1 < G:
                        stats(LN_B[nxt])
                    dve.wait_ge(rows_in[R_D[blk] % 2], 16 * (R_D[blk] // 2 + 1))
                    with steps.loop(0, A // 2, 2) as i:
                        for par in range(2):
                            down_out(g, s, 2 * i + par, b, par)

        @block.tensor
        def _(pe):
            def transpose_x(m, a_blocks, x_=xa):
                pe.wait_ge(xn_ready, m + 1)
                for k in range(K):
                    if k < 2:
                        reach(pe, h32_ready, K * m)
                        reach(pe, x2_ready, K * a_blocks)
                    else:
                        pe.wait_ge(h32_ready, K * m + k - 1)
                    for a in range(A):
                        ins = nc.tensor.transpose(bank(TB[k % 2])[:, a * P:(a + 1) * P],
                                                  x_[:, a, k * P:(k + 1) * P], ident[:])
                    ins.then_inc(xt_ready, 1)

            def project(n, m, y_before):
                pe.wait_ge(lo_ready, K * (m + 1))
                reach(pe, o_ready, y_before)
                for a in range(A):
                    reach(pe, q_taken, A * n + max(a - 1, 0))
                    for k in range(K):
                        for i, (wp, hp) in enumerate(SPLIT):
                            ins = nc.tensor.matmul(bank(QY[a % 2]), hq[hp][:, k, a * P:(a + 1) * P], WQ[wp][:, k],
                                                   start=(k == 0 and i == 0), stop=(k == K - 1 and i == 2))
                    ins.then_inc(q_ready, 1)

            def transpose_g(n, m):
                pe.wait_ge(g_ready, n + 1)
                pe.wait_ge(h32_ready, K * (m + 1))
                for k in range(K):
                    if k >= 2:
                        pe.wait_ge(x2_ready, K * n + k - 1)
                    for a in range(A):
                        ins = nc.tensor.transpose(bank(TB[k % 2])[:, a * P:(a + 1) * P],
                                                  H[:, a, k * P:(k + 1) * P], ident[:])
                    ins.then_inc(gt_ready, 1)

            def gate_up(g, j, s):
                u = (g * J + j) * S + s
                reach(pe, hd_ready, u - 1)
                for t in range(2):
                    for k in range(K):
                        for i, (wp, hp) in enumerate(SPLIT):
                            at = (2 * j + t) * BLK + k * P
                            ins = nc.tensor.matmul(bank(GU[2 * s + t]), W[wp][:, bass.ds(at, P)], h2[hp][:, s, k],
                                                   start=(k == 0 and i == 0), stop=(k == K - 1 and i == 2))
                ins.then_inc(gu_ready, 1)

            def down(g, s, q, par):
                d = (g * S + s) * A + q
                reach(pe, o_ready, d - 1 if g or s or par else d)
                for j in range(J):
                    for i, (wp, hp) in enumerate(SPLIT):
                        at = (j * S + s) * BLK + q * P
                        w_at = (2 * J + j) * BLK
                        ins = nc.tensor.matmul(bank(QY[par]), hid[hp][:, bass.ds(at, P)], W[wp][:, w_at:w_at + BLK],
                                               start=(j == 0 and i == 0), stop=(j == J - 1 and i == 2))
                ins.then_inc(y_ready, 1)

            def mod_vec(sections, slot):
                for s in sections:
                    pe.wait_ge(mod_in[s], 16)
                    for kb in range(K):
                        at = (slot(s) * K + kb) * BATCH
                        for k in range(K):
                            ins = nc.tensor.matmul(bank(QY[1])[:, at:at + BATCH], mod_w[s][:, k, kb * P:(kb + 1) * P],
                                                   cT[:, k], start=k == 0, stop=k == K - 1)
                ins.then_inc(vec_mm, 1)

            def mod_row(s, first):
                pe.wait_ge(mod_in[s], 16)
                for b in range(BATCH):
                    for k in range(K):
                        ins = nc.tensor.matmul(bank(GU[first + b]), cT[:, k, b:b + 1].broadcast_to((P, P)),
                                               mod_w[s][:, k], start=k == 0, stop=k == K - 1)
                    ins.then_inc(row_mm, 1)

            pe.wait_ge(silu_c, 1)
            pe.wait_ge(id_ready, 1)
            mod_vec((SA, CA, GA), lambda s: s)
            mod_row(GA, 0)

            pe.wait_ge(wq_ready, 1)
            transpose_x(0, 0)
            with pe.Fori(0, NB - 1) as q:
                project(q, q, 0)
                transpose_x(q + 1, q)
                transpose_g(q, q + 1)
            project(NB - 1, NB - 1, 0)
            transpose_g(NB - 1, NB - 1)
            pe.wait_ge(q_taken, A * NB)
            mod_vec((SB, CB), lambda s: s)
            mod_row(GB, 2)
            pe.wait_ge(vec_ready, 2)
            transpose_x(LN_B[0], NB)

            for g in range(G):
                if g == 0:
                    for s in range(S):
                        if s:
                            transpose_x(LN_B[s], NB, H)
                        pe.wait_ge(lo_ready, K * (LN_B[s] + 1))
                        gate_up(g, 0, s)
                    with pe.Fori(1, J) as j:
                        pe.wait_ge(w_built, 2 * j + 2)
                        for s in range(S):
                            gate_up(g, j, s)
                    pe.wait_ge(w_built, NCH + 1)
                else:
                    pe.wait_ge(lo_ready, K * (LN_B[S * g + 1] + 1))
                if g == 1:
                    for s in range(S):
                        gate_up(g, 0, s)
                    transpose_x(LN_A[NB], NB)
                    for s in range(S):
                        gate_up(g, 1, s)

                    def attn_block(q, last):
                        n, m = NB + q, LN_A[NB] + q
                        project(n, m, A * S * g)
                        gate_up(g, 2 + 2 * q, 0)
                        if not last:
                            transpose_x(m + 1, n)
                        gate_up(g, 2 + 2 * q, 1)
                        gate_up(g, 3 + 2 * q, 0)
                        transpose_g(n, m if last else m + 1)
                        gate_up(g, 3 + 2 * q, 1)

                    with pe.Fori(0, NB - 1) as q:
                        attn_block(q, False)
                    attn_block(NB - 1, True)
                    for s in range(S):
                        gate_up(g, J - 1, s)
                if g > 1:
                    with pe.Fori(0, J) as j:
                        for s in range(S):
                            gate_up(g, j, s)
                pe.wait_ge(hid_ready, (g + 1) * J * S)
                for s in range(S):
                    down(g, s, 0, 0)
                    down(g, s, 1, 1)
                    if g + 1 < G:
                        transpose_x(LN_B[(g + 1) * S + s], NB if g < 1 else 2 * NB)
                    down(g, s, 2, 0)
                    down(g, s, 3, 1)


_INS = {"x": "L0_attn_X", "wq": "L0_attn_W_Q", "hh_b": "L0_attn_hh_b", "lut": "L0_ffn_lut", "wmod": "L0_wmod"}


def chunks(gate_idx, up_idx, down_idx):
    def padded(a):
        return np.concatenate([a, np.zeros((J * P - F,) + a.shape[1:], a.dtype)])

    def by_channel(a):
        return padded(a).reshape(J, P, K, P).transpose(0, 3, 2, 1)

    down = padded(np.ascontiguousarray(down_idx.T)).reshape(J, P, K * P)
    gate_up = np.stack([by_channel(gate_idx), by_channel(up_idx)], axis=1).reshape(2 * J, P, BLK)
    return np.concatenate([gate_up, down])


def rope_tables():
    e = (np.arange(0, ROPE, 2, dtype=np.float32) / np.float32(ROPE)).astype(np.float64)
    inv_freq = (1 / (np.float64(10000) ** e).astype(np.float32)).astype(np.float32)
    angle = np.arange(T, dtype=np.float32)[:, None] * inv_freq[None, :]
    lay = lambda a: np.ascontiguousarray(
        a.astype(np.float32).reshape(T // P, P, ROPE // 2).transpose(1, 0, 2).reshape(P, -1))
    return lay(np.cos(angle.astype(np.float64))), lay(np.sin(angle.astype(np.float64)))


def kernel(**inputs):
    import concourse.bacc as bacc
    from concourse.bass_utils import run_bass_kernel_spmd as run

    nc = bacc.Bacc("TRN2", target_bir_lowering=False, num_devices=1)
    a = {k: np.ascontiguousarray(inputs[v]) for k, v in _INS.items()}
    by_part = lambda v: np.ascontiguousarray(np.asarray(v).reshape(-1, P).T)
    a["gn_w"], a["gn_b"] = by_part(inputs["L0_attn_gn_weight"]), by_part(inputs["L0_attn_gn_bias"])
    a["c_t"] = np.ascontiguousarray(np.asarray(inputs["L0_c"]).reshape(BATCH, K, P).transpose(2, 1, 0))
    a["idx"] = chunks(*(np.asarray(inputs[f"L0_ffn_{n}_idx"]) for n in ("gate", "up", "down")))
    a["cos"], a["sin"] = rope_tables()
    aps = {k: nc.dram_tensor(f"{k}_dram", v.shape, mybir.dt.from_np(v.dtype), kind="ExternalInput").ap()
           for k, v in a.items()}
    out = nc.dram_tensor("out_dram", (BATCH, T, C), F32, kind="ExternalOutput").ap()
    build(nc, **aps, out=out)
    r = run(nc, [{f"{k}_dram": v for k, v in a.items()}], core_ids=[0])
    return r.results[0]["out_dram"]
```

```python
from contextlib import ExitStack, contextmanager

import numpy as np

import concourse.bass as bass
from concourse import mybir

F32 = mybir.dt.float32
F16 = mybir.dt.float16
I32 = mybir.dt.int32
ALU = mybir.AluOpType
ACT = mybir.ActivationFunctionType
AX = mybir.AxisListType.X
RMAX = bass.bass_isa.ReduceOp.max

P = 128
BATCH, T, C = 2, 2048, 512
BLK = 512
A = BLK // P
K = C // P
NB = T // BLK
F = 1376
J = -(-F // P)
F_LAST = F - (J - 1) * P
GRP, GSZ = 32, 16
ROPE = 64
S = 2
G = BATCH * NB // S
LUT = 16
EPS = 1e-5
RSQRT_SEED = float(0x5F3759DF)
EXP1 = float(1 << 23)
SA, CA, GA, SB, CB, GB = range(6)
NCH = 3 * J
AHEAD = 4
SUMMED = AHEAD * NB + 6
POOL_PAIRS = 2
V, HALF = LUT // 2, P // 2
SPLIT = ((0, 0), (0, 1), (1, 0))


class Steps:

    def __init__(self, eng, sem):
        self.eng, self.sem, self.base, self.n = eng, sem, 0, 0

    def mark(self, ins):
        ins.then_inc(self.sem, 1)
        self.n += 1

    def wait(self):
        self.eng.wait_ge(self.sem, self.base + self.n)

    def step(self, ins):
        self.mark(ins)
        self.wait()

    @contextmanager
    def loop(self, first, end, per):
        start = self.base + self.n
        with self.eng.Fori(first, end) as i:
            self.base, self.n = start + (i - first) * per, 0
            yield i
            assert self.n == per, self.n
        self.base, self.n = start + (end - first) * per, 0


def reach(eng, sem, value):
    if not isinstance(value, int) or value > 0:
        eng.wait_ge(sem, value)


def build(nc, x, wq, hh_b, gn_w, gn_b, lut, idx, c_t, wmod, cos, sin, out):
    x2_dram = nc.dram_tensor("x2_dram", (BATCH, NB, P, A * C), F32, kind="Internal").ap()
    x_toks = x.rearrange("b (m a p) n -> b m p a n", p=P, a=A)
    x2_rows = x2_dram.rearrange("b m p (q n) -> b m p q n", q=A)
    out_rows = out.rearrange("b (m p q) n -> b m p q n", p=P, q=A)

    with ExitStack() as ctx:
        def sb(name, shape, dt):
            return ctx.enter_context(nc.sbuf_tensor(name, shape, dt))

        def sem(name):
            return ctx.enter_context(nc.semaphore(name))

        w_all = sb("w_all", [P, 2 * NCH * BLK], F16)
        W = [w_all[:, h * NCH * BLK:(h + 1) * NCH * BLK] for h in range(2)]
        MOD_AT = (0, 8, NCH, 16, NCH + 16, NCH + 24)
        DIAG_AT = 24
        mod_w = [w_all[:, at * BLK:at * BLK + 2 * K * C].bitcast(F32).rearrange("p (k n) -> p k n", k=K)
                 for at in MOD_AT]
        diag = w_all[:, DIAG_AT * BLK:DIAG_AT * BLK + V * P].rearrange("p (v n) -> p v n", v=V)
        hid = [sb(f"hid{h}", [P, J * S * BLK], F16) for h in range(2)]
        h2 = [sb(f"h2_{h}", [P, S, K, BLK], F16) for h in range(2)]
        work = sb("work", [P, 2 * A * C], F32)
        H = work[:, 0:A * C].rearrange("p (a n) -> p a n", a=A)
        hq_all = work[:, A * C:2 * A * C].bitcast(F16)
        hq = [hq_all[:, h * K * BLK:(h + 1) * K * BLK].rearrange("p (k n) -> p k n", k=K) for h in range(2)]
        R = [sb(f"R{i}", [P, A * C], F32) for i in range(2)]
        xa = sb("xa", [P, A, C], F32)
        h32 = sb("h32", [P, 2, BLK], F32)
        sq = sb("sq", [P, 2, BLK], F32)
        WQ = [sb(f"WQ{h}", [P, K, C], F16) for h in range(2)]
        cosT = sb("cosT", [P, T // P * (ROPE // 2)], F32)
        sinT = sb("sinT", [P, T // P * (ROPE // 2)], F32)
        hhS = sb("hhS", [P, C], F32)
        gaB = sb("gaB", [P, BATCH, C], F32)
        gbB = sb("gbB", [P, BATCH, C], F32)
        sg = sb("sg", [P, S, BLK], F32)
        ident = sb("ident", [P, P], F32)
        vec = sb("vec", [P, 5, K, BATCH], F32)
        gnw = sb("gnw", [P, K], F32)
        gnb = sb("gnb", [P, K], F32)
        cT = sb("cT", [P, K, BATCH], F32)
        lutS = sb("lutS", [P, LUT], F32)
        lutH = sb("lutH", [P, 2, LUT], F32)
        lut16 = sb("lut16", [P, LUT], F16)
        lutQ = sb("lutQ", [P, 2, LUT // 2], F32)
        esel = sb("esel", [P, P // 2], F32)
        shift = sb("shift", [P, 1], F32)
        lutD = sb("lutD", [P, LUT // 2], F32)
        st = sb("st", [P, A, 6], F32)
        mv = sb("mv", [P, A, 2], F32)
        ls = sb("ls", [P, 5, A], F32)
        gs = sb("gs", [P, 4, A * GRP], F32)
        col = sb("col", [P, 16], F32)
        hd = sb("hd", [P, S, BLK], F32)
        ps = ctx.enter_context(nc.psum_tensor("ps", [P, 8 * BLK], F32))

        def bank(i):
            return ps[:, i * BLK:(i + 1) * BLK]

        GU, TB, QY = (0, 1, 2, 3), (4, 5), (6, 7)

        def part(t, i):
            return t[:, i * BLK:(i + 1) * BLK]

        onehot = [hid[i][:, 0:LUT * BLK].rearrange("p (v h n) -> p v h n", v=V, h=2) for i in range(2)]
        idx_sum = [hid[i][:, LUT * BLK:(LUT + 4) * BLK].bitcast(I32).rearrange("p (h n) -> p h n", h=2)
                   for i in range(2)]
        idx16 = [hid[i][:, (LUT + 4) * BLK:(LUT + 6) * BLK].rearrange("p (h n) -> p h n", h=2) for i in range(2)]
        h2_f32 = h2[0].rearrange("p s k n -> p (s k n)").bitcast(F32)
        bias_rows = [[part(h2_f32, i) for i in range(2)],
                     [hid[i][:, (J - 1) * S * BLK:].bitcast(F32) for i in range(2)]]
        idx_sel = [h32[:, i].bitcast(I32) for i in range(2)]
        bit = [sq[:, i].bitcast(I32) for i in range(2)]
        mask = [xa[:, i].bitcast(I32) for i in range(3)]
        pairs = [[part(work, g) for g in range(8)], [part(R[g // 4], g % 4) for g in range(8)]]

        (c_wqmax, c_wqall, c_sq, c_isq, c_s, c_is, c_sh, c_kappa, c_kappa2, c_e, c_tmp) = \
            (col[:, i:i + 1] for i in range(11))

        def idx_loaded(w, par):
            if isinstance(w, int) and w < SUMMED:
                return 16 * (w - par) + 32
            return 8 * (w - par) + 16 + 8 * SUMMED

        x_in = sem("x_in"); x_in_h = sem("x_in_h"); rows_in = [sem("rows_in0"), sem("rows_in1")]
        wq_in = sem("wq_in"); const_in = sem("const_in"); rope_in = sem("rope_in")
        mod_in = [sem(f"mod_in{s}") for s in range(6)]
        idx_in = [sem("idx_in0"), sem("idx_in1")]
        x2_out = sem("x2_out"); x2_rest = sem("x2_rest"); y_out = [sem("y_out0"), sem("y_out1")]
        id_zero = sem("id_zero"); id_ready = sem("id_ready"); wq_all = sem("wq_all")
        dstep = sem("dstep")
        silu_c = sem("silu_c"); vec_mm = sem("vec_mm"); row_mm = sem("row_mm")
        vec_ready = sem("vec_ready"); row_ready = sem("row_ready")
        wq_max = sem("wq_max"); wq_ready = sem("wq_ready")
        ln_stats = sem("ln_stats"); xn_ready = sem("xn_ready"); xt_ready = sem("xt_ready")
        h32_ready = sem("h32_ready"); hi_ready = sem("hi_ready"); lo_ready = sem("lo_ready")
        q_ready = sem("q_ready"); q_taken = sem("q_taken"); pre_tanh = sem("pre_tanh"); tanh_ready = sem("tanh_ready")
        centered = sem("centered"); squared = sem("squared"); sq_summed = sem("sq_summed")
        g_ready = sem("g_ready"); gt_ready = sem("gt_ready"); x2_ready = sem("x2_ready")
        lut_split = sem("lut_split"); esel_ready = sem("esel_ready"); diag_ready = sem("diag_ready")
        idx_used = sem("idx_used"); idx16_ready = sem("idx16_ready")
        onehot_ready = sem("onehot_ready"); w_sum = sem("w_sum")
        rows_bias = sem("rows_bias"); rows_added = sem("rows_added")
        bit_ready = sem("bit_ready"); w_hi = sem("w_hi"); pool_pairs = sem("pool_pairs")
        pairs_ready = sem("pairs_ready"); w_built = sem("w_built")
        gu_ready = sem("gu_ready"); silu_ready = sem("silu_ready"); hd_ready = sem("hd_ready")
        hid_hi_ready = sem("hid_hi_ready"); hid_ready = sem("hid_ready")
        y_ready = sem("y_ready"); o_ready = sem("o_ready")

        block = ctx.enter_context(nc.Block())

        SELECT_AFTER = [u * 7 // 4 for u in range(NCH - SUMMED)]

        LN_A = [0, 1, 2, 3, 8, 9, 10, 11]
        LN_B = [4, 5, 6, 7, 12, 13, 14, 15]
        R_A = [0, 1, 2, 3, 6, 7, 8, 9]
        R_D = [4, 5, 10, 11, 12, 13, 14, 15]

        @block.sync
        def _(sp):
            def load_x(src, m, tile=xa):
                reach(sp, xt_ready, K * m if tile is xa else 0)
                sp.dma_start(tile[:], src).then_inc(x_in if tile is xa else x_in_h, 16)

            def load_idx(w, par):
                if isinstance(w, int) and w < SUMMED:
                    reach(sp, idx16_ready, w - 1)
                    for d in range(2):
                        sp.dma_start(idx_sum[par][d * HALF:(d + 1) * HALF],
                                     idx[w].rearrange("(h p) n -> p h n", h=2)).then_inc(idx_in[par], 16)
                else:
                    reach(sp, idx_used, w - 1 - SUMMED)
                    sp.dma_start(idx_sel[par], idx[w] if isinstance(w, int) else
                                 idx[bass.ds(w, 1)].squeeze(0)).then_inc(idx_in[par], 16)

            def load_rows(r, src):
                sp.dma_start(R[r].rearrange("p (q n) -> p q n", q=A), src).then_inc(rows_in[r], 16)

            def rows_of_block(b, q):
                return x.rearrange("b (m p q) n -> b q p m n", p=P, q=A)[b, q]

            def x2_of_block(b, q):
                return x2_dram.rearrange("b m p (q n) -> b q p m n", q=A)[b, q]

            sp.dma_start(cT[:], c_t).then_inc(const_in, 16)
            sp.dma_start(lutS[:], lut.partition_broadcast(P)).then_inc(const_in, 16)
            sp.dma_start(hhS[:], hh_b.partition_broadcast(P)).then_inc(const_in, 16)
            sp.dma_start(gnw[:], gn_w).then_inc(const_in, 16)
            sp.dma_start(gnb[:], gn_b).then_inc(const_in, 16)
            wq_f32 = hid[0][:, 0:2 * K * C].bitcast(F32).rearrange("p (k n) -> p k n", k=K)
            mod_v = wmod.rearrange("(k p) (s n) -> s p k n", p=P, s=6)

            def load_mod(s):
                sp.dma_start(mod_w[s], mod_v[s]).then_inc(mod_in[s], 16)

            load_mod(SA)
            sp.dma_start(wq_f32, wq.rearrange("(k p) n -> p k n", p=P)).then_inc(wq_in, 16)
            load_mod(CA)
            load_x(x_toks[0, 0], 0)
            load_idx(0, 0)
            load_idx(1, 1)
            load_mod(GA)
            sp.dma_start(cosT[:], cos).then_inc(rope_in, 16)
            sp.dma_start(sinT[:], sin).then_inc(rope_in, 16)
            load_rows(0, rows_of_block(0, 0))
            for s in (SB, CB, GB):
                load_mod(s)
            for w in range(2, AHEAD):
                load_idx(w, w % 2)

            for q in range(NB):
                if q + 1 < NB:
                    load_x(x_toks[0, q + 1], q + 1)
                    reach(sp, x2_out, 16 * q)
                    load_rows((q + 1) % 2, rows_of_block(0, q + 1))
                last = q == NB - 1
                for w in range(AHEAD * (q + 1), AHEAD * (q + 2) - last):
                    load_idx(w, w % 2)
                if not last:
                    sp.wait_ge(x2_ready, K * (q + 1))
                    sp.dma_start(x2_of_block(0, q), R[q % 2].rearrange("p (q n) -> p q n", q=A)).then_inc(x2_out, 16)
                else:
                    for k in range(K):
                        sp.wait_ge(x2_ready, K * q + k + 1)
                        sp.dma_start(x2_rows[0, k][:, q], R[q % 2][:, k * C:(k + 1) * C]) \
                          .then_inc(x2_rest if k else x2_out, 16)
            sp.wait_ge(x2_out, 16 * NB)
            load_x(x2_rows[0, 0], LN_B[0])
            load_idx(AHEAD * (NB + 1) - 1, 1)
            sp.wait_ge(x2_rest, 16 * (K - 1))
            load_x(x2_rows[0, 1], LN_B[1], H)
            for w in range(AHEAD * (NB + 1), SUMMED):
                load_idx(w, w % 2)
            sp.wait_ge(lo_ready, K * (LN_B[1] + 1))
            for w in (SUMMED, SUMMED + 1):
                load_idx(w, w % 2)
            with sp.Fori(SUMMED // 2 + 1, NCH // 2) as i:
                for par in range(2):
                    load_idx(2 * i + par, par)
            load_idx(NCH - 1, 0)

            def load_ffn_block(blk):
                load_x(x2_rows[blk // NB, blk % NB], LN_B[blk])

            def out_rows_of(g, s, first):
                blk = g * S + s
                with sp.Fori(first, first + A // 2) as q:
                    sp.wait_ge(o_ready, blk * A + q + 1)
                    sp.dma_start(out_rows[blk // NB, blk % NB, :, bass.ds(q, 1), :].squeeze(1),
                                 R[R_D[blk] % 2][:, bass.ds(q * C, C)]).then_inc(y_out[R_D[blk] % 2], 16)

            def down_io(g):
                for s in range(S):
                    out_rows_of(g, s, 0)
                    if g + 1 < G and s == 0:
                        load_ffn_block((g + 1) * S + 1)
                    if g == 0 and s == 1:
                        load_x(x_toks[1, 0], LN_A[NB])
                    if g == 1 and s == 1:
                        load_ffn_block(3 * S)
                    out_rows_of(g, s, A // 2)

            def load_down_rows(g, s):
                blk = g * S + s
                if g >= 2:
                    sp.wait_ge(y_out[R_D[blk] % 2], 16 * A * (blk // 2))
                load_rows(R_D[blk] % 2, x2_rows[blk // NB, blk % NB])

            for g in range(G):
                if g == 0:
                    sp.wait_ge(w_built, NCH)
                    load_ffn_block(S)
                if g == 1:
                    for q in range(NB):
                        n = NB + q
                        if q == 0:
                            sp.wait_ge(y_out[R_A[n] % 2], 16 * A)
                            load_rows(R_A[n] % 2, rows_of_block(1, 0))
                        if q + 1 < NB:
                            load_x(x_toks[1, q + 1], LN_A[n] + 1)
                            if q == 0:
                                sp.wait_ge(y_out[R_A[n + 1] % 2], 16 * A)
                            reach(sp, x2_out, 16 * n)
                            load_rows(R_A[n + 1] % 2, rows_of_block(1, q + 1))
                        sp.wait_ge(x2_ready, K * (n + 1))
                        sp.dma_start(x2_of_block(1, q), R[R_A[n] % 2].rearrange("p (q n) -> p q n", q=A)) \
                          .then_inc(x2_out, 16)
                    sp.wait_ge(x2_out, 16 * BATCH * NB)
                    load_ffn_block(2 * S)
                for s in range(S):
                    load_down_rows(g, s)
                down_io(g)
            for r in range(2):
                sp.wait_ge(y_out[r], 16 * A * BATCH * NB // 2)

        @block.gpsimd
        def _(pool):
            nc.gpsimd.memset(ident[:], 0.0).then_inc(id_zero, 1)
            pool.wait_ge(id_zero, 1)
            nc.gpsimd.affine_select(out=ident[:], in_=ident[:], compare_op=ALU.not_equal, fill=1.0, base=0,
                                    pattern=[[-1, P]], channel_multiplier=1).then_inc(id_ready, 1)
            pool.wait_ge(id_ready, 1)
            nc.gpsimd.tensor_tensor(esel[:], ident[:, 0:HALF], ident[:, HALF:P], ALU.add).then_inc(esel_ready, 1)
            pool.wait_ge(esel_ready, 1)
            pool.wait_ge(lut_split, 1)
            for h in range(2):
                for v_ in range(V):
                    ins = nc.gpsimd.tensor_scalar(diag[:, v_, h * HALF:(h + 1) * HALF], esel[:],
                                                  lutQ[:, h, v_:v_ + 1], None, ALU.mult)
            ins.then_inc(diag_ready, 1)
            pool.wait_ge(wq_max, 1)
            nc.gpsimd.partition_all_reduce(c_wqall, c_wqmax, P, RMAX).then_inc(wq_all, 1)

            def split_lo(m, hi, lo):
                for k in range(K):
                    pool.wait_ge(hi_ready, K * m + k + 1)
                    nc.gpsimd.tensor_tensor(lo[:, k], h32[:, k % 2], hi[:, k], ALU.subtract).then_inc(lo_ready, 1)

            def half_idx(w, par):
                reach(pool, onehot_ready, w - 1)
                pool.wait_ge(idx_in[par], idx_loaded(w, par))
                nc.gpsimd.tensor_scalar(idx16[par], idx_sum[par], shift[:], None, ALU.add).then_inc(idx16_ready, 1)

            def some_pairs(w, par):
                pool.wait_ge(bit_ready, w - SUMMED + 1)
                pool.wait_ge(w_built, w - 1)
                for g in range(POOL_PAIRS):
                    ins = nc.gpsimd.tensor_scalar(pairs[par][g], bit[par], lutD[:, g:g + 1],
                                                  lutS[:, 2 * g:2 * g + 1], ALU.mult, ALU.add)
                ins.then_inc(pool_pairs, 1)

            def table_lo(w, par):
                pool.wait_ge(w_hi, w - SUMMED + 1)
                hi, lo = (W[h][:, bass.ds(w * BLK, BLK)] for h in range(2))
                nc.gpsimd.tensor_tensor(lo, pairs[par][0], hi, ALU.subtract).then_inc(w_built, 1)

            def add_bias_rows(n, b):
                r = R_A[n] % 2
                pool.wait_ge(rows_in[r], 16 * (R_A[n] // 2 + 1))
                for k in range(K):
                    Rk, bias = R[r][:, k * C:(k + 1) * C], bias_rows[b][k % 2]
                    reach(pool, rows_added, K * n + k - 1)
                    nc.gpsimd.tensor_scalar(bias, gaB[:, b], gnb[:, k:k + 1], None, ALU.mult).then_inc(rows_bias, 1)
                    pool.wait_ge(rows_bias, K * n + k + 1)
                    nc.gpsimd.tensor_tensor(Rk, Rk, bias, ALU.add).then_inc(rows_added, 1)

            half_idx(0, 0)
            half_idx(1, 1)
            split_lo(0, hq[0], hq[1])
            half_idx(2, 0)
            for q in range(NB - 1):
                w = AHEAD * q + AHEAD // 2
                half_idx(w + 1, 1)
                if q == 0:
                    pool.wait_ge(row_ready, 1)
                add_bias_rows(q, 0)
                half_idx(w + 2, 0)
                split_lo(q + 1, hq[0], hq[1])
                half_idx(w + 3, 1)
                half_idx(w + 4, 0)
            half_idx(AHEAD * NB - 1, 1)
            add_bias_rows(NB - 1, 0)
            for w in range(AHEAD * NB, SUMMED):
                half_idx(w, w % 2)
            split_lo(LN_B[0], h2[0][:, 0], h2[1][:, 0])
            split_lo(LN_B[1], h2[0][:, 1], h2[1][:, 1])
            some_pairs(SUMMED, SUMMED % 2)
            w = SUMMED
            for u in range(S * J):
                at = u * BLK
                pool.wait_ge(hid_hi_ready, u + 1)
                nc.gpsimd.tensor_tensor(hid[1][:, at:at + BLK], hd[:, u % S], hid[0][:, at:at + BLK],
                                        ALU.subtract).then_inc(hid_ready, 1)
                if u in SELECT_AFTER and w + 1 < NCH:
                    some_pairs(w + 1, (w + 1) % 2)
                if u in SELECT_AFTER:
                    table_lo(w, w % 2)
                    w += 1
            for g in range(G):
                if g == 1:
                    split_lo(LN_A[NB], hq[0], hq[1])
                    for n in range(NB, 2 * NB):
                        add_bias_rows(n, 1)
                        if n + 1 < 2 * NB:
                            split_lo(LN_A[n + 1], hq[0], hq[1])
                if g + 1 < G:
                    for s in range(S):
                        split_lo(LN_B[(g + 1) * S + s], h2[0][:, s], h2[1][:, s])

        @block.scalar
        def _(act):
            def norm(m, x_=xa):
                act.wait_ge(ln_stats, m + 1)
                for a in range(A):
                    ins = nc.scalar.activation(x_[:, a], x_[:, a], ACT.Identity,
                                               bias=ls[:, 3, a:a + 1], scale=ls[:, 2, a:a + 1])
                ins.then_inc(xn_ready, 1)

            def affine(m, scale, shift, b, dest, dest_free, banks=TB, halves=(0, 1)):
                for k2 in (2 * h for h in halves):
                    for k in (k2, k2 + 1):
                        act.wait_ge(xt_ready, K * m + k + 1)
                        reach(act, lo_ready, K * m + max(k - 1, 0))
                        nc.scalar.activation(h32[:, k % 2], bank(banks[k % len(banks)]), ACT.Identity,
                                             bias=vec[:, shift, k, b:b + 1], scale=vec[:, scale, k, b:b + 1]) \
                          .then_inc(h32_ready, 1)
                    for k in (k2, k2 + 1):
                        act.wait_ge(h32_ready, K * m + k + 1)
                        if k == 0:
                            dest_free()
                        nc.scalar.activation(dest[:, k], h32[:, k % 2], ACT.Copy).then_inc(hi_ready, 1)

            def tanh(n, a):
                act.wait_ge(pre_tanh, A * n + a + 1)
                nc.scalar.activation(H[:, a], H[:, a], ACT.Tanh, scale=c_isq).then_inc(tanh_ready, 1)

            def square(n, a):
                act.wait_ge(centered, A * n + a + 1)
                reach(act, sq_summed, A * n + max(a - 1, 0))
                nc.scalar.activation(sq[:, a % 2], H[:, a], ACT.Square).then_inc(squared, 1)

            def silu(g, j, s):
                u = (g * J + j) * S + s
                act.wait_ge(gu_ready, u + 1)
                reach(act, hd_ready, u - 1)
                nc.scalar.activation(sg[:, s], bank(GU[2 * s]), ACT.Silu, scale=c_is).then_inc(silu_ready, 1)

            def hid_hi(g, j, s):
                u = (g * J + j) * S + s
                act.wait_ge(hd_ready, u + 1)
                nc.scalar.activation(hid[0][:, bass.ds((j * S + s) * BLK, BLK)], hd[:, s], ACT.Copy) \
                  .then_inc(hid_hi_ready, 1)

            def summed_out(w, par):
                act.wait_ge(w_sum, w + 1)
                for half in range(2):
                    rows = slice(half * HALF, (half + 1) * HALF)
                    for h in range(2):
                        ins = nc.scalar.activation(W[h][rows, bass.ds(w * BLK, BLK)],
                                                   bank(GU[2 * par + half])[h * HALF:(h + 1) * HALF], ACT.Copy)
                ins.then_inc(w_built, 1)

            def pair_tables(w, par):
                act.wait_ge(bit_ready, w - SUMMED + 1)
                act.wait_ge(w_built, w - 1)
                for g in range(POOL_PAIRS, 8):
                    ins = nc.scalar.activation(pairs[par][g], bit[par], ACT.Identity,
                                               bias=lutS[:, 2 * g:2 * g + 1], scale=lutD[:, g:g + 1])
                ins.then_inc(pairs_ready, 1)

            act.wait_ge(const_in, 80)
            nc.scalar.activation(cT[:], cT[:], ACT.Silu).then_inc(silu_c, 1)

            norm(0)
            act.wait_ge(vec_ready, 1)
            affine(0, CA, SA, 0, hq[0], lambda: None)

            def attn_block(q, last):
                w = AHEAD * q
                tanh(q, 0); tanh(q, 1); square(q, 0); tanh(q, 2); square(q, 1)
                if not last:
                    norm(q + 1)
                tanh(q, 3)
                summed_out(w, 0)
                square(q, 2); square(q, 3)
                summed_out(w + 1, 1)
                if not last:
                    affine(q + 1, CA, SA, 0, hq[0], lambda: act.wait_ge(q_ready, A * q + A))
                summed_out(w + 2, 0)
                summed_out(w + 3, 1)

            with act.Fori(0, NB - 1) as q:
                attn_block(q, False)
            attn_block(NB - 1, True)

            w = AHEAD * NB
            summed_out(w, 0)
            summed_out(w + 1, 1)
            act.wait_ge(vec_ready, 2)
            summed_out(w + 2, 0)
            norm(LN_B[0])
            affine(LN_B[0], CB, SB, 0, h2[0][:, 0], lambda: None)
            norm(LN_B[1], H)
            for h in range(2):
                affine(LN_B[1], CB, SB, 0, h2[0][:, 1], lambda: None, halves=(h,))
                summed_out(w + 3 + h, 1 - h)
            summed_out(w + 5, 1)

            silu(0, 0, 0)
            pair_tables(SUMMED, SUMMED % 2)
            w = SUMMED + 1
            for u in range(S * J):
                hid_hi(0, u // S, u % S)
                if u + 1 < S * J:
                    silu(0, (u + 1) // S, (u + 1) % S)
                if u in SELECT_AFTER and w < NCH:
                    pair_tables(w, w % 2)
                    w += 1

            def gate_units(g, first, end):
                with act.Fori(first, end) as j:
                    for s in range(S):
                        silu(g, j, s)
                        hid_hi(g, j, s)

            for g in range(G):
                if g == 1:
                    norm(LN_A[NB])
                    gate_units(g, 0, 1)
                    affine(LN_A[NB], CA, SA, 1, hq[0], lambda: None)
                    gate_units(g, 1, 2)

                    def attn_unit_silu(q, i):
                        silu(g, 2 + 2 * q + i // S, i % S)

                    def attn_unit_hi(q, i):
                        hid_hi(g, 2 + 2 * q + i // S, i % S)

                    def attn_block(q, last):
                        n, m = NB + q, LN_A[NB] + q
                        tanh(n, 0); tanh(n, 1); square(n, 0); tanh(n, 2); square(n, 1)
                        if not last:
                            norm(m + 1)
                        tanh(n, 3)
                        attn_unit_silu(q, 0)
                        square(n, 2)
                        attn_unit_silu(q, 1)
                        for h in range(2):
                            if not last:
                                affine(m + 1, CA, SA, 1, hq[0], lambda: act.wait_ge(q_ready, A * n + A), halves=(h,))
                            if h == 0:
                                square(n, 3)
                        attn_unit_hi(q, 0); attn_unit_hi(q, 1)
                        for i in range(2, 2 * S):
                            attn_unit_silu(q, i); attn_unit_hi(q, i)

                    with act.Fori(0, NB - 1) as q:
                        attn_block(q, False)
                    attn_block(NB - 1, True)
                    gate_units(g, 2 + 2 * NB, J)
                if g > 1:
                    gate_units(g, 0, J)
                if g + 1 < G:
                    for s in range(S):
                        blk = (g + 1) * S + s
                        norm(LN_B[blk])
                        affine(LN_B[blk], CB, SB, blk // NB, h2[0][:, s], lambda: None, GU)

        @block.vector
        def _(dve):
            steps = Steps(dve, dstep)
            step = steps.step
            v = nc.vector

            def alone():
                v.memset(col[:, 15:16], 0.0)

            def rsqrt(x_, t_, y_, masks_par=None):
                steps.mark(v.tensor_scalar(y_.bitcast(I32), x_.bitcast(I32), -0.5, RSQRT_SEED, ALU.mult, ALU.add))
                for i in range(9):
                    if masks_par is not None and i < V:
                        entry_mask(masks_par, i)
                    steps.wait()
                    if i % 3 == 0:
                        ins = v.tensor_tensor(t_, y_, y_, ALU.mult)
                    elif i % 3 == 1:
                        ins = v.scalar_tensor_tensor(t_, t_, -0.5, x_, ALU.mult, ALU.mult)
                    else:
                        ins = v.scalar_tensor_tensor(y_, t_, 1.5, y_, ALU.add, ALU.mult)
                    steps.mark(ins)
                steps.wait()

            def stats(m, x_=xa):
                if x_ is xa:
                    late = not isinstance(m, int) or m > LN_B[1]
                    dve.wait_ge(x_in, 16 * m + (0 if late else 16))
                else:
                    dve.wait_ge(x_in_h, 16)
                for a in range(A):
                    ins = v.bn_stats(st[:, a], x_[:, a])
                step(ins)
                alone()
                for a in range(A):
                    ins = v.bn_aggr(mv[:, a], st[:, a])
                step(ins)
                reach(dve, xn_ready, m)
                step(v.tensor_scalar(ls[:, 0], mv[:, :, 1], EPS, None, ALU.add))
                rsqrt(ls[:, 0], ls[:, 1], ls[:, 2])
                v.scalar_tensor_tensor(ls[:, 3], mv[:, :, 0], -1.0, ls[:, 2], ALU.mult, ALU.mult) \
                 .then_inc(ln_stats, 1)

            def rope_relu(n, q, a):
                reach(dve, pre_tanh, A * n + a)
                dve.wait_ge(q_ready, A * n + a + 1)
                Q = bank(QY[a % 2])
                half = ROPE // 2
                at = (q * A + a) * half
                cs, sn = cosT[:, bass.ds(at, half)], sinT[:, bass.ds(at, half)]
                Qr = Q[:, 0:ROPE].rearrange("p (i e) -> p e i", e=2)
                rot2 = gs2[:, 0:ROPE].rearrange("p (i e) -> p e i", e=2)
                tmp2 = gs2[:, ROPE:2 * ROPE].rearrange("p (i e) -> p e i", e=2)
                both = lambda t: t.unsqueeze(1).broadcast_to((P, 2, half))
                v.tensor_tensor(rot2, Qr, both(cs), ALU.mult)
                step(v.tensor_tensor(tmp2, Qr, both(sn), ALU.mult))
                v.tensor_tensor(rot2[:, 0], rot2[:, 0], tmp2[:, 1], ALU.subtract)
                step(v.tensor_tensor(rot2[:, 1], rot2[:, 1], tmp2[:, 0], ALU.add))
                v.scalar_tensor_tensor(H[:, a, ROPE:], Q[:, ROPE:], 0.0, hhS[:, ROPE:], ALU.max, ALU.add) \
                 .then_inc(q_taken, 1)
                v.scalar_tensor_tensor(H[:, a, 0:ROPE], gs2[:, 0:ROPE], 0.0, hhS[:, 0:ROPE],
                                       ALU.max, ALU.add).then_inc(pre_tanh, 1)

            def center(n, a):
                dve.wait_ge(tanh_ready, A * n + a + 1)
                Hg = H[:, a].rearrange("p (g e) -> p g e", e=GSZ)
                sums = gs[:, 0, a * GRP:(a + 1) * GRP]
                step(v.tensor_reduce(sums, Hg, axis=AX, op=ALU.add))
                v.scalar_tensor_tensor(Hg, sums.unsqueeze(2).broadcast_to((P, GRP, GSZ)), -1.0 / GSZ, Hg,
                                       ALU.mult, ALU.add) \
                 .then_inc(centered, 1)

            def sum_squares(n, a):
                dve.wait_ge(squared, A * n + a + 1)
                v.tensor_reduce(gs[:, 1, a * GRP:(a + 1) * GRP], sq[:, a % 2].rearrange("p (g e) -> p g e", e=GSZ),
                                axis=AX, op=ALU.add).then_inc(sq_summed, 1)

            def group_scale(n, b, masks_par=None):
                dve.wait_ge(sq_summed, A * n + A)
                step(v.tensor_scalar(gs[:, 1], gs[:, 1], 1.0 / GSZ, EPS, ALU.mult, ALU.add))
                rsqrt(gs[:, 1], gs[:, 2], gs[:, 3], masks_par)
                r = gs[:, 3].rearrange("p (a g) -> p a g", a=A)
                ga = vec[:, GA, :, b].unsqueeze(2).broadcast_to((P, A, GRP))
                step(v.tensor_tensor(r, r, ga, ALU.mult))
                Hg = H.rearrange("p a (g e) -> p (a g) e", e=GSZ)
                v.tensor_tensor(Hg, Hg, gs[:, 3].unsqueeze(2).broadcast_to((P, A * GRP, GSZ)), ALU.mult) \
                 .then_inc(g_ready, 1)

            def residual(n, r):
                dve.wait_ge(rows_added, K * (n + 1))
                for k in range(K):
                    Rk = R[r][:, k * C:(k + 1) * C]
                    dve.wait_ge(gt_ready, K * n + k + 1)
                    v.scalar_tensor_tensor(Rk, bank(TB[k % 2]), gnw[:, k:k + 1], Rk, ALU.mult, ALU.add) \
                     .then_inc(x2_ready, 1)

            def masks(w, par):
                masks_free(w)
                for v_ in range(V):
                    entry_mask(par, v_)

            def masks_free(w):
                reach(dve, w_sum, w - 1)
                dve.wait_ge(idx16_ready, w + 1)

            def entry_mask(par, v_):
                ins = v.tensor_scalar(onehot[par][:, v_], idx16[par], float(v_), None, ALU.is_equal)
                if v_ == V - 1:
                    ins.then_inc(onehot_ready, 1)

            def low_bit(w, par):
                dve.wait_ge(idx_in[par], idx_loaded(w, par))
                v.tensor_scalar(bit[par], idx_sel[par], 1, None, ALU.bitwise_and).then_inc(bit_ready, 1)

            def build_chunk(w, par, more=True):
                for i in range(3):
                    ins = v.tensor_scalar(mask[i], idx_sel[par], 2 << i, None, ALU.bitwise_and)
                ins.then_inc(idx_used, 1)
                if more:
                    low_bit(w + 1, 1 - par)
                dve.wait_ge(idx_used, w - SUMMED + 1)
                dve.wait_ge(pairs_ready, w - SUMMED + 1)
                dve.wait_ge(pool_pairs, w - SUMMED + 1)
                g = pairs[par]
                for level, span in ((0, 1), (1, 2), (2, 4)):
                    alone()
                    for at in range(0, 8, 2 * span):
                        ins = v.copy_predicated(g[at], mask[level], g[at + span])
                    step(ins)
                v.tensor_scalar(W[0][:, bass.ds(w * BLK, BLK)], g[0], 1.0, None, ALU.mult).then_inc(w_hi, 1)

            def hidden(g, j, s):
                u = (g * J + j) * S + s
                reach(dve, hid_ready, u - 1)
                dve.wait_ge(silu_ready, u + 1)
                v.scalar_tensor_tensor(hd[:, s], bank(GU[2 * s + 1]), c_kappa, sg[:, s], ALU.mult, ALU.mult) \
                 .then_inc(hd_ready, 1)

            def hid_lo(g, j, s):
                u = (g * J + j) * S + s
                dve.wait_ge(hid_hi_ready, u + 1)
                at = bass.ds((j * S + s) * BLK, BLK)
                v.tensor_tensor(hid[1][:, at], hd[:, s], hid[0][:, at], ALU.subtract).then_inc(hid_ready, 1)

            def down_out(g, s, q, b, par):
                d = (g * S + s) * A + q
                r = R_D[g * S + s] % 2
                dve.wait_ge(y_ready, d + 1)
                step(v.scalar_tensor_tensor(hd[:, par], bank(QY[par]), c_kappa2, gbB[:, b], ALU.mult, ALU.mult))
                Rq = R[r][:, bass.ds(q * C, C)]
                v.tensor_tensor(Rq, hd[:, par], Rq, ALU.add).then_inc(o_ready, 1)

            dve.wait_ge(const_in, 80)
            gs2 = gs[:, 2]

            def magnitude(dst, src):
                step(v.tensor_scalar(dst.bitcast(I32), src.bitcast(I32), 0x7FFFFFFF, None, ALU.bitwise_and))

            def exponent(dst, src, lowest, highest):
                step(v.tensor_scalar(dst.bitcast(I32), src.bitcast(I32), 0x7F800000, None, ALU.bitwise_and))
                step(v.tensor_scalar(dst.bitcast(I32), dst.bitcast(I32), lowest * EXP1, highest * EXP1,
                                     ALU.max, ALU.min))

            def field(dst, src, times, plus):
                step(v.tensor_scalar(dst.bitcast(I32), src.bitcast(I32), float(times), plus * EXP1,
                                     ALU.mult, ALU.add))

            tmp16 = gs[:, 0, 0:LUT]
            magnitude(tmp16, lutS[:])
            step(v.tensor_reduce(c_tmp, tmp16, axis=AX, op=ALU.max))
            exponent(c_e, c_tmp, 60, 186)
            field(c_s, c_e, -1, 264)
            field(c_is, c_s, -1, 254)
            field(c_sh, c_e, -2, 374)
            field(c_tmp, c_sh, -1, 254)
            step(v.tensor_tensor(c_kappa, c_is, c_sh, ALU.mult))
            step(v.tensor_tensor(c_kappa2, c_is, c_tmp, ALU.mult))
            step(v.tensor_scalar(lutS[:], lutS[:], c_s, None, ALU.mult))
            lp = lutS.rearrange("p (g e) -> p e g", e=2)
            v.tensor_tensor(lutD[:], lp[:, 1], lp[:, 0], ALU.subtract)

            step(v.tensor_scalar(lut16[:], lutS[:], 1.0, None, ALU.mult))
            step(v.tensor_scalar(lutH[:, 0], lut16[:], 1.0, None, ALU.mult))
            step(v.tensor_tensor(lutH[:, 1], lutS[:], lutH[:, 0], ALU.subtract))
            for d in range(2):
                v.memset(shift[d * HALF:(d + 1) * HALF], -float(d * V))
                ins = v.tensor_copy(lutQ[d * HALF:(d + 1) * HALF], lutH[d * HALF:(d + 1) * HALF, :, d * V:(d + 1) * V])
            ins.then_inc(lut_split, 1)

            wq_f32 = hid[0][:, 0:2 * K * C].bitcast(F32)
            wq_s = hid[1][:, 0:2 * K * C].bitcast(F32)
            dve.wait_ge(wq_in, 16)
            magnitude(wq_s, wq_f32)
            v.tensor_reduce(c_wqmax, wq_s, axis=AX, op=ALU.max).then_inc(wq_max, 1)
            stats(0)
            dve.wait_ge(wq_all, 1)
            exponent(c_e, c_wqall, 60, 186)
            field(c_sq, c_e, -1, 264)
            field(c_isq, c_sq, -1, 254)
            v.tensor_scalar(hhS[:], hhS[:], c_sq, None, ALU.mult)
            step(v.tensor_scalar(wq_s, wq_f32, c_sq, None, ALU.mult))
            step(v.tensor_scalar(WQ[0].rearrange("p k n -> p (k n)"), wq_s, 1.0, None, ALU.mult))
            v.tensor_tensor(WQ[1].rearrange("p k n -> p (k n)"), wq_s, WQ[0].rearrange("p k n -> p (k n)"),
                            ALU.subtract).then_inc(wq_ready, 1)

            vps = bank(QY[1])[:, 0:5 * K * BATCH].rearrange("p (s k b) -> p s k b", s=5, k=K)

            gate_ps = bank(GU[3])[:, 0:5 * K * BATCH].rearrange("p (s k b) -> p s k b", s=5, k=K)

            def gate_of(dst, src, tmp, tmp2):
                v.tensor_scalar(tmp, src, 0.0, 2.0, ALU.is_ge, ALU.mult)
                magnitude(tmp2, src)
                step(v.tensor_scalar(tmp2, tmp2, 0.25, None, ALU.max))
                return v.scalar_tensor_tensor(dst, tmp, 1.0, tmp2, ALU.subtract, ALU.mult)

            dve.wait_ge(vec_mm, 1)
            v.tensor_copy(vec[:, SA], vps[:, SA])
            v.tensor_scalar(vec[:, CA], vps[:, CA], 1.0, None, ALU.add).then_inc(vec_ready, 1)
            dve.wait_ge(rope_in, 32)

            def gates_of_attn():
                dve.wait_ge(vec_mm, 2)
                flat = lambda t: t.rearrange("p k b -> p (k b)")
                step(gate_of(flat(vec[:, GA]), flat(gate_ps[:, GA]), gs[:, 3, 0:K * BATCH],
                             gs[:, 3, K * BATCH:2 * K * BATCH]))
                for b in range(BATCH):
                    dve.wait_ge(row_mm, b + 1)
                    step(gate_of(gaB[:, b], bank(GU[b]), hd[:, 0], hd[:, 1]))
                    ins = v.memset(col[:, 14:15], 0.0)
                ins.then_inc(row_ready, 1)

            masks(0, 0)
            gates_of_attn()

            def scales_of_ffn():
                dve.wait_ge(vec_mm, 3)
                v.tensor_copy(vec[:, SB], vps[:, SB])
                v.tensor_scalar(vec[:, CB], vps[:, CB], 1.0, None, ALU.add).then_inc(vec_ready, 1)

            def attn_block(q, half, last):
                w = AHEAD * q
                masks(w + 1, 1)
                rope_relu(q, q, 0); rope_relu(q, q, 1); center(q, 0); rope_relu(q, q, 2); center(q, 1)
                if not last:
                    stats(q + 1)
                rope_relu(q, q, 3)
                sum_squares(q, 0); center(q, 2); sum_squares(q, 1); center(q, 3)
                if not last:
                    masks(w + 2, 0)
                sum_squares(q, 2); sum_squares(q, 3)
                if last:
                    group_scale(q, 0)
                    masks(w + 2, 0)
                else:
                    masks_free(w + 3)
                    group_scale(q, 0, 1)
                    masks(w + 4, 0)
                if q == NB - 2:
                    scales_of_ffn()
                residual(q, half)
                if last:
                    masks(w + 3, 1)
                    masks(w + 4, 0)

            for q in range(NB):
                attn_block(q, q % 2, q == NB - 1)

            w = AHEAD * NB
            masks(w + 1, 1)
            masks(w + 2, 0)
            stats(LN_B[0])
            masks(w + 3, 1)
            stats(LN_B[1], H)
            masks(w + 4, 0)
            masks(w + 5, 1)
            for b in range(BATCH):
                dve.wait_ge(row_mm, BATCH + b + 1)
                step(gate_of(gbB[:, b], bank(QY[b]), hd[:, 0], hd[:, 1]))

            low_bit(SUMMED, SUMMED % 2)
            w = SUMMED
            for u in range(S * J):
                hidden(0, u // S, u % S)
                if u in SELECT_AFTER:
                    build_chunk(w, w % 2, w + 1 < NCH)
                    w += 1
            dve.wait_ge(w_built, NCH)
            for h in range(2):
                ins = v.memset(W[h][F_LAST:P, (NCH - 1) * BLK:], 0.0)
            ins.then_inc(w_built, 1)

            def gate_units(g, first, end):
                with steps.loop(first, end, 0) as j:
                    for s in range(S):
                        hidden(g, j, s)
                        hid_lo(g, j, s)

            for g in range(G):
                b = g * S // NB
                if g == 1:
                    stats(LN_A[NB])
                    gate_units(g, 0, 2)

                    def attn_hidden(q, i):
                        hidden(g, 2 + 2 * q + i // S, i % S)

                    def attn_lo(q, i):
                        hid_lo(g, 2 + 2 * q + i // S, i % S)

                    def attn_block(q, half, last):
                        n, m = NB + q, LN_A[NB] + q
                        rope_relu(n, q, 0); rope_relu(n, q, 1); center(n, 0); rope_relu(n, q, 2); center(n, 1)
                        if not last:
                            stats(m + 1)
                        rope_relu(n, q, 3)
                        sum_squares(n, 0); center(n, 2); sum_squares(n, 1); center(n, 3)
                        attn_hidden(q, 0)
                        sum_squares(n, 2); sum_squares(n, 3)
                        attn_hidden(q, 1)
                        group_scale(n, 1)
                        attn_lo(q, 0); attn_lo(q, 1)
                        attn_hidden(q, 2); attn_lo(q, 2)
                        residual(n, half)
                        attn_hidden(q, 3); attn_lo(q, 3)

                    for q in range(NB):
                        attn_block(q, q % 2, q == NB - 1)
                    gate_units(g, 2 + 2 * NB, J)
                if g > 1:
                    gate_units(g, 0, J)
                for s in range(S):
                    blk, nxt = g * S + s, (g + 1) * S + s
                    if g + 1 < G:
                        stats(LN_B[nxt])
                    dve.wait_ge(hid_ready, (g + 1) * J * S)
                    dve.wait_ge(rows_in[R_D[blk] % 2], 16 * (R_D[blk] // 2 + 1))
                    with steps.loop(0, A // 2, 2) as i:
                        for par in range(2):
                            down_out(g, s, 2 * i + par, b, par)

        @block.tensor
        def _(pe):
            def transpose_x(m, a_blocks, x_=xa, banks=TB):
                pe.wait_ge(xn_ready, m + 1)
                for k in range(K):
                    if k == 0:
                        reach(pe, h32_ready, K * m)
                        reach(pe, x2_ready, K * a_blocks)
                    if k >= len(banks):
                        pe.wait_ge(h32_ready, K * m + k - 1)
                    for a in range(A):
                        ins = nc.tensor.transpose(bank(banks[k % len(banks)])[:, a * P:(a + 1) * P],
                                                  x_[:, a, k * P:(k + 1) * P], ident[:])
                    ins.then_inc(xt_ready, 1)

            def project(n, m, y_before):
                pe.wait_ge(lo_ready, K * (m + 1))
                reach(pe, o_ready, y_before)
                for a in range(A):
                    reach(pe, q_taken, A * n + max(a - 1, 0))
                    for k in range(K):
                        for i, (wp, hp) in enumerate(SPLIT):
                            ins = nc.tensor.matmul(bank(QY[a % 2]), hq[hp][:, k, a * P:(a + 1) * P], WQ[wp][:, k],
                                                   start=(k == 0 and i == 0), stop=(k == K - 1 and i == 2))
                    ins.then_inc(q_ready, 1)

            def transpose_g(n, m):
                pe.wait_ge(g_ready, n + 1)
                pe.wait_ge(h32_ready, K * (m + 1))
                for k in range(K):
                    if k >= 2:
                        pe.wait_ge(x2_ready, K * n + k - 1)
                    for a in range(A):
                        ins = nc.tensor.transpose(bank(TB[k % 2])[:, a * P:(a + 1) * P],
                                                  H[:, a, k * P:(k + 1) * P], ident[:])
                    ins.then_inc(gt_ready, 1)

            def sum_chunk(w, par, first=False):
                pe.wait_ge(onehot_ready, w + 1)
                reach(pe, w_built, w if first else w - 1)
                for half in range(2):
                    for v_ in range(V):
                        ins = nc.tensor.matmul(bank(GU[2 * par + half]), diag[:, v_], onehot[par][:, v_, half],
                                               start=v_ == 0, stop=v_ == V - 1)
                ins.then_inc(w_sum, 1)

            def gate_up(g, j, s):
                u = (g * J + j) * S + s
                reach(pe, hd_ready, u - 1)
                for t in range(2):
                    for k in range(K):
                        for i, (wp, hp) in enumerate(SPLIT):
                            at = (2 * j + t) * BLK + k * P
                            ins = nc.tensor.matmul(bank(GU[2 * s + t]), W[wp][:, bass.ds(at, P)], h2[hp][:, s, k],
                                                   start=(k == 0 and i == 0), stop=(k == K - 1 and i == 2))
                ins.then_inc(gu_ready, 1)

            def down(g, s, q, par, first=False):
                d = (g * S + s) * A + q
                reach(pe, o_ready, d - 1 if g or s or par else d)
                for j in range(J):
                    if first and j == J - 1:
                        pe.wait_ge(hid_ready, (g + 1) * J * S - S + s + 1)
                    for i, (wp, hp) in enumerate(SPLIT):
                        at = (j * S + s) * BLK + q * P
                        w_at = (2 * J + j) * BLK
                        ins = nc.tensor.matmul(bank(QY[par]), hid[hp][:, bass.ds(at, P)], W[wp][:, w_at:w_at + BLK],
                                               start=(j == 0 and i == 0), stop=(j == J - 1 and i == 2))
                ins.then_inc(y_ready, 1)

            def mod_vec(sections, to=QY[1]):
                if sections[0] == SB:
                    pe.wait_ge(q_taken, A * (NB - 1))
                for s in sections:
                    pe.wait_ge(mod_in[s], 16)
                    for kb in range(K):
                        at = (s * K + kb) * BATCH
                        for k in range(K):
                            ins = nc.tensor.matmul(bank(to)[:, at:at + BATCH], mod_w[s][:, k, kb * P:(kb + 1) * P],
                                                   cT[:, k], start=k == 0, stop=k == K - 1)
                ins.then_inc(vec_mm, 1)

            def mod_row(s, banks):
                if banks is QY:
                    pe.wait_ge(q_taken, A * NB)
                pe.wait_ge(mod_in[s], 16)
                for b in range(BATCH):
                    for k in range(K):
                        ins = nc.tensor.matmul(bank(banks[b]), cT[:, k, b:b + 1].broadcast_to((P, P)),
                                               mod_w[s][:, k], start=k == 0, stop=k == K - 1)
                    ins.then_inc(row_mm, 1)

            pe.wait_ge(silu_c, 1)
            pe.wait_ge(id_ready, 1)
            mod_vec((SA, CA))
            mod_vec((GA,), GU[3])
            transpose_x(0, 0)
            mod_row(GA, GU)
            pe.wait_ge(wq_ready, 1)
            pe.wait_ge(diag_ready, 1)

            def attn_block(q, last=False, scales=False):
                w = AHEAD * q
                project(q, q, 0)
                sum_chunk(w, 0, True)
                sum_chunk(w + 1, 1)
                if last:
                    mod_row(GB, QY)
                    transpose_g(q, q)
                else:
                    transpose_x(q + 1, q)
                sum_chunk(w + 2, 0)
                if scales:
                    mod_vec((SB, CB))
                sum_chunk(w + 3, 1)
                if not last:
                    transpose_g(q, q + 1)

            pe.wait_ge(row_ready, 1)
            with pe.Fori(0, NB - 2) as q:
                attn_block(q)
            attn_block(NB - 2, scales=True)
            pe.wait_ge(vec_ready, 2)
            attn_block(NB - 1, last=True)
            w = AHEAD * NB
            for i in range(3):
                sum_chunk(w + i, i % 2)
            transpose_x(LN_B[0], NB)
            sum_chunk(w + 3, 1)
            transpose_x(LN_B[1], NB, H)
            sum_chunk(w + 4, 0)
            sum_chunk(w + 5, 1)
            pe.wait_ge(w_built, SUMMED)

            for g in range(G):
                if g == 0:
                    for s in range(S):
                        pe.wait_ge(lo_ready, K * (LN_B[s] + 1))
                        gate_up(g, 0, s)
                    with pe.Fori(1, J) as j:
                        pe.wait_ge(w_built, 2 * j + 2)
                        for s in range(S):
                            gate_up(g, j, s)
                    pe.wait_ge(w_built, NCH + 1)
                else:
                    pe.wait_ge(lo_ready, K * (LN_B[S * g + 1] + 1))
                if g == 1:
                    gate_up(g, 0, 0)
                    gate_up(g, 0, 1)
                    gate_up(g, 1, 0)
                    transpose_x(LN_A[NB], NB)
                    gate_up(g, 1, 1)

                    def attn_block(q, last):
                        n, m = NB + q, LN_A[NB] + q
                        project(n, m, A * S * g)
                        gate_up(g, 2 + 2 * q, 0)
                        gate_up(g, 2 + 2 * q, 1)
                        if not last:
                            transpose_x(m + 1, n)
                        gate_up(g, 3 + 2 * q, 0)
                        gate_up(g, 3 + 2 * q, 1)
                        transpose_g(n, m if last else m + 1)

                    with pe.Fori(0, NB - 1) as q:
                        attn_block(q, False)
                    attn_block(NB - 1, True)
                    for s in range(S):
                        gate_up(g, J - 1, s)
                if g > 1:
                    with pe.Fori(0, J) as j:
                        for s in range(S):
                            gate_up(g, j, s)
                pe.wait_ge(hid_ready, (g + 1) * J * S - S)
                for s in range(S):
                    down(g, s, 0, 0, True)
                    down(g, s, 1, 1)
                    if g + 1 < G:
                        pe.wait_ge(hd_ready, (g + 1) * J * S)
                        transpose_x(LN_B[(g + 1) * S + s], NB if g < 1 else 2 * NB, banks=GU)
                    down(g, s, 2, 0)
                    down(g, s, 3, 1)


_INS = {"x": "L0_attn_X", "wq": "L0_attn_W_Q", "hh_b": "L0_attn_hh_b", "lut": "L0_ffn_lut", "wmod": "L0_wmod"}


def chunks(gate_idx, up_idx, down_idx):
    def padded(a):
        return np.concatenate([a, np.zeros((J * P - F,) + a.shape[1:], a.dtype)])

    def by_channel(a):
        return padded(a).reshape(J, P, K, P).transpose(0, 3, 2, 1)

    down = padded(np.ascontiguousarray(down_idx.T)).reshape(J, P, K * P)
    gate_up = np.stack([by_channel(gate_idx), by_channel(up_idx)], axis=1).reshape(2 * J, P, BLK)
    return np.concatenate([gate_up, down])


def rope_tables():
    e = (np.arange(0, ROPE, 2, dtype=np.float32) / np.float32(ROPE)).astype(np.float64)
    inv_freq = (1 / (np.float64(10000) ** e).astype(np.float32)).astype(np.float32)
    angle = np.arange(T, dtype=np.float32)[:, None] * inv_freq[None, :]
    lay = lambda a: np.ascontiguousarray(
        a.astype(np.float32).reshape(T // P, P, ROPE // 2).transpose(1, 0, 2).reshape(P, -1))
    return lay(np.cos(angle.astype(np.float64))), lay(np.sin(angle.astype(np.float64)))


def kernel(**inputs):
    import concourse.bacc as bacc
    from concourse.bass_utils import run_bass_kernel_spmd as run

    nc = bacc.Bacc("TRN2", target_bir_lowering=False, num_devices=1)
    a = {k: np.ascontiguousarray(inputs[v]) for k, v in _INS.items()}
    by_part = lambda v: np.ascontiguousarray(np.asarray(v).reshape(-1, P).T)
    a["gn_w"], a["gn_b"] = by_part(inputs["L0_attn_gn_weight"]), by_part(inputs["L0_attn_gn_bias"])
    a["c_t"] = np.ascontiguousarray(np.asarray(inputs["L0_c"]).reshape(BATCH, K, P).transpose(2, 1, 0))
    a["idx"] = chunks(*(np.asarray(inputs[f"L0_ffn_{n}_idx"]) for n in ("gate", "up", "down")))
    a["cos"], a["sin"] = rope_tables()
    aps = {k: nc.dram_tensor(f"{k}_dram", v.shape, mybir.dt.from_np(v.dtype), kind="ExternalInput").ap()
           for k, v in a.items()}
    out = nc.dram_tensor("out_dram", (BATCH, T, C), F32, kind="ExternalOutput").ap()
    build(nc, **aps, out=out)
    r = run(nc, [{f"{k}_dram": v for k, v in a.items()}], core_ids=[0])
    return r.results[0]["out_dram"]
```
